# Optimizing a Trainium2 kernel written in Bass

```python
import numpy as np
import jax
import jax.numpy as jnp

def _softmax(x, axis=-1):
    return jax.nn.softmax(x, axis=axis)
def _gelu(x):
    return jax.nn.gelu(x, approximate=True)
def _silu(x):
    return jax.nn.silu(x)
def _sigmoid(x):
    return jax.nn.sigmoid(x)
def _layernorm(x, axis=-1, eps=1e-5):
    m = jnp.mean(x, axis=axis, keepdims=True)
    v = jnp.var(x, axis=axis, keepdims=True)
    return (x - m) / jnp.sqrt(v + eps)
def _scatter_add(tgt, idx, src, axis=0):
    return tgt.at[idx].add(src)
def _segment_sum(src, seg, n):
    return jax.ops.segment_sum(src, seg, n)

kernel_name = 'mk_adj_preln_d1_adj_512_574e9b'

def setup_inputs(seed: int = 0):
    np.random.seed(seed)
    _w = jnp.asarray
    def _rec_inputs():
        import jax
        import jax.numpy as jnp
        _gk = jax.random.key(seed)
        x = -0.0005963 + 1.001 * jax.random.normal(jax.random.fold_in(_gk, 1), (6144, 512), jnp.float32)
        _w = (1.0 + jnp.arange(6144, dtype=jnp.float32)) ** -0.5
        _w = _w / _w.mean()
        _pij = jnp.clip(0.00130208 * _w[:, None] * _w[None, :], 0.0, 1.0)
        _a = jax.random.uniform(jax.random.fold_in(_gk, 2), (6144, 6144)) < _pij
        adj = _a.astype(jnp.int32)
        return x, adj
    x, adj = _rec_inputs()
    def _L0_gnn_setup():
        import jax, jax.numpy as jnp
        import numpy as np
        N = 6144
        IN_F = 512
        H = 8
        DH = 64
        ALPHA = 0.2
        NEG = -1000000000.0
        key = jax.random.key(seed)
        k1, k2, k3, k4, k5 = jax.random.split(key, 5)
        x = jax.random.normal(k1, (N, IN_F), dtype=jnp.float32)
        adj = jax.random.randint(k2, (N, N), 0, 2, dtype=jnp.int32)
        W = jax.random.normal(k3, (H * DH, IN_F), dtype=jnp.float32) * (2.0 / (IN_F + H * DH)) ** 0.5
        b = jnp.zeros((H * DH,), dtype=jnp.float32)
        aw = jax.random.normal(k4, (H, DH, 2), dtype=jnp.float32) * (2.0 / (DH + 2)) ** 0.5
        return {'x': x, 'adj': adj, 'W': W, 'b': b, 'aw': aw}
    _L0_gnn_all = _L0_gnn_setup()
    _L0_gnn_in = {k: v for k, v in _L0_gnn_all.items() if k in ('W', 'b', 'aw', )}
    del _L0_gnn_all

    return {
        "x": x,
        "adj": adj,
        "L0_gnn_W": _L0_gnn_in["W"],
        "L0_gnn_b": _L0_gnn_in["b"],
        "L0_gnn_aw": _L0_gnn_in["aw"],
    }

def reference(x, adj, L0_gnn_W, L0_gnn_b, L0_gnn_aw):
    import jax
    import jax.numpy as jnp
    def _L0_gnn_ref(x, adj, W, b, aw):
        import jax, jax.numpy as jnp
        import numpy as np
        N = 6144
        IN_F = 512
        H = 8
        DH = 64
        ALPHA = 0.2
        NEG = -1000000000.0
        h = (x @ W.T + b).reshape(N, H, DH).transpose(1, 0, 2)
        a = jnp.einsum('hnd,hdk->hnk', h, aw)
        scores = jax.nn.leaky_relu(a[:, :, 0][:, :, None] + a[:, :, 1][:, None, :], ALPHA)
        mask = (adj > 0)[None, :, :]
        scores = jnp.where(mask, scores, NEG)
        p = jax.nn.softmax(scores, axis=2)
        p = jnp.where(mask, p, 0.0)
        out = jnp.einsum('hij,hjd->hid', p, h)
        out = out.transpose(1, 0, 2).reshape(N, H * DH)
        return out

    h = jnp.maximum(_layernorm(x, axis=-1), 0.0)
    x = x + _L0_gnn_ref(h, adj, L0_gnn_W, L0_gnn_b, L0_gnn_aw)
    return x


_drawn_inputs = setup_inputs


def setup_inputs(seed=0):
    import zlib

    import numpy as np

    out = dict(_drawn_inputs(seed))
    spreads = {'L0_gnn_b': (0.0, 0.1)}
    factors = {}
    for name, (base, spread) in spreads.items():
        noise = np.random.default_rng([zlib.crc32(name.encode()), seed]).standard_normal(out[name].shape)
        drawn = base * np.exp(spread * noise) if base else spread * noise
        out[name] = jnp.asarray(drawn.astype(out[name].dtype))
    for name, factor in factors.items():
        out[name] = (out[name] * factor).astype(out[name].dtype)
    return out
```

```python
import concourse.bass as bass
from concourse import mybir
from contextlib import ExitStack


N, D, H, DH = 6144, 512, 8, 64
P = 128
NT = N // P
KC = D // P
BITS = 8
NW = N // BITS
NCH = 16
CW = NW // NCH
LW = 40
K = 48
TOP = 8192
WSC = 1024
NV = NCH + NT - 1
NVP = NV + 1
VC = 2 + 2 * H + K
TR = D + H
PE_ = 256
NB = P * K // PE_
NMAX = 1536
LAG = 2
RING = 4
QMAX = -(-(NCH * NB + (NT - 1) * (P * LW // PE_)) // RING)
ALPHA = 0.2
HEADROOM = 40.0
GONE = -3.0e5
FAR = -1.0e30


def constants():
    import numpy as np

    f = np.float32
    eye = np.eye(P, dtype=f)
    c = {}
    c["eye"] = eye
    w = np.arange(NW)
    c["wordrow"] = np.stack([w // 256 * 256, w % 256]).astype(f)
    c["bitmask"] = np.tile((1 << (11 + np.arange(BITS))).astype(np.int32), (P, 1))
    c["bitcol"] = np.tile((NW * np.arange(BITS)).astype(f), (P, 1))
    c["count"] = np.tile(np.arange(PE_).astype(f), (P, 1))
    c["batchbase"] = np.tile((PE_ * np.arange(NB)).astype(f), (P, 1))
    e = np.arange(P)[:, None]
    c["flatpos"] = (e + P * np.arange(2 * NB)[None, :]).astype(f)
    c["before"] = (np.arange(P)[:, None] < np.arange(P)[None, :]).astype(f)
    c["diff"] = eye - np.eye(P, k=1, dtype=f)
    c["upto"] = (np.arange(P)[:, None] <= np.arange(P)[None, :]).astype(f)
    c["row"] = np.arange(P, dtype=f)[:, None].copy()
    c["steps"] = np.tile(np.arange(NMAX + 1).astype(f), (NV, 1))
    v = np.arange(NV)
    c["newrow"] = (v >= NCH - 1).astype(f)[:, None].copy()
    c["ones"] = np.ones((P, P), f)
    return c


def build(nc, x, adj, W, b, aw, const, out):
    f32, bf16, i32 = mybir.dt.float32, mybir.dt.bfloat16, mybir.dt.int32
    ALU, ACT, AX = mybir.AluOpType, mybir.ActivationFunctionType, mybir.AxisListType
    table = nc.dram_tensor("table", [N, TR], f32).ap()

    ctx = ExitStack()
    with ctx:
        def sb(name, shape, dt):
            return ctx.enter_context(nc.sbuf_tensor(name, shape, dt))

        def pb(name, shape):
            return ctx.enter_context(nc.psum_tensor(name, shape, f32))

        def sem(name):
            return ctx.enter_context(nc.semaphore(name))

        C = {k: sb("c_" + k, list(const[k].shape), const[k].dtype) for k in const}
        eye = C["eye"]
        packs = sb("packs", [P, BITS, P], bf16)
        wordrow = sb("wordrow", [2, NW], bf16)
        ones2 = sb("ones2", [2, P], bf16)

        xt = sb("xt", [P, 2, D], f32)
        hn = sb("hn", [P, D], f32)
        ht = sb("ht", [P, KC, P], f32)
        wraw = sb("wraw", [P, KC, D], f32)
        wt = sb("wt", [P, KC, D], f32)
        aw2 = sb("aw2", [P, KC, 2], f32)
        awd = sb("awd", [P, KC, 2 * H], f32)
        wa = sb("wa", [P, KC, 2 * H], f32)
        bcol = sb("bcol", [P, KC], f32)
        bias = sb("bias", [P, D], f32)
        biasrep = sb("biasrep", [P, KC, P], f32)
        abias = sb("abias", [P, 2 * H], f32)
        stats = sb("stats", [P, 2, 6], f32)
        mv = sb("mv", [P, 2, 2], f32)
        negm = sb("negm", [P, 2], f32)
        sd = sb("sd", [P, 2], f32)
        rs = sb("rs", [P, 2], f32)
        epsc = sb("epsc", [P, 1], f32)
        halfc = sb("halfc", [P, 1], f32)
        trow = sb("trow", [P, 2, TR], f32)
        ab = sb("ab", [P, NT, 2 * H], f32)
        aj = sb("aj", [P, 2, N], i32)
        sg = sb("sg", [P, 2, N], bf16)
        signsum = sb("signsum", [P, NT], f32)
        tops = sb("tops", [P, NCH * 8], f32)
        wl = sb("wl", [P, LW], f32)
        wint = sb("wint", [P, CW], i32)
        widx = sb("widx", [P, CW], i32)
        wneg = sb("wneg", [P, CW], f32)
        bits = sb("bits", [P, BITS, CW], i32)
        cand = sb("cand", [P, BITS, CW], f32)
        lst = sb("lst", [P, K], f32)
        V = sb("V", [P, NVP, VC], f32)
        Dv = sg[:, 0:2, :].rearrange("p a n -> p (a n)")[:, 0:2 * NVP * VC].bitcast(f32).rearrange("p (v c) -> p v c", c=VC)
        starts = sb("starts", [P, NVP], f32)
        bmax1 = sb("bmax1", [P, H], f32)
        bmax = sb("bmax", [P, H], f32)
        bound = sb("bound", [P, NT, H], f32)
        cnt = sb("cnt", [P, NV], f32)
        cnt0 = sb("cnt0", [P, 1], f32)
        miss = sb("miss", [P, NT], f32)
        missmax = sb("missmax", [P, NT], f32)
        missi = sb("missi", [P, NT], i32)
        edges = sb("edges", [NV, 1], f32)
        nbi = sb("nbi", [NV, 1], i32)
        nb = sb("nb", [NV, 1], f32)
        cum = sb("cum", [NV, 1], f32)
        sched = sb("sched", [1, 4, NMAX], i32)
        vrow = sb("vrow", [1, 512], f32)
        iters = sb("iters", [1, 1], i32)
        reach = sb("reach", [P, RING, PE_], f32)
        rank = sb("rank", [P, 2], f32)
        hit = sb("hit", [P, 2, K], f32)
        pick = sb("pick", [P, 2, K], f32)
        val = sb("val", [P, 2], f32)
        live = sb("live", [P, 2], f32)
        idx = sb("idx", [P, RING, 2], i32)
        sel = sb("sel", [P, RING, 2, P], f32)
        G = aj[:, 0, 0:RING * 2 * TR].bitcast(f32).rearrange("p (g c) -> p g c", c=TR)
        Y = aj[:, 1, 0:RING * 2 * D].bitcast(f32).rearrange("p (g c) -> p g c", c=D)
        z = sb("z", [P, 2, H], f32)
        z2 = sb("z2", [P, 2, H], f32)
        adj4 = aj[:, 0, :]
        sign4 = sg[:, 0, :]
        G4 = aj[:, 1, 0:8 * TR].bitcast(f32).rearrange("p (g c) -> p g c", c=TR)
        l8 = sb("l8", [P, 8], f32)
        pen8 = sb("pen8", [P, 8], f32)
        idx8 = sb("idx8", [P, 8], i32)
        z8 = sb("z8", [P, 8, H], f32)
        prob8 = sb("prob8", [P, 8, H], f32)
        most = sb("most", [P, 1], f32)
        count4 = sb("count4", [P, 1], f32)
        steps4 = sb("steps4", [1, 1], i32)
        prob = sb("prob", [P, RING, 2, H], f32)
        zero = sb("zero", [P, P], bf16)
        zrow = sb("zrow", [P, D], bf16)
        xo = sb("xo", [P, D], f32)
        ob = sb("ob", [P, D], f32)
        den = sb("den", [P, H], f32)
        rden = sb("rden", [P, H], f32)

        psT, psH, psA, psD = pb("psT", [P, 512]), pb("psH", [P, 512]), pb("psA", [P, 512]), pb("psD", [P, 512])
        psW = pb("psW", [P, 1024])
        psX = pb("psX", [P, 512])
        psY = pb("psY", [P, 512])
        psS = psD
        fetchd = [psT, psH, psX, psY]

        reachn = reach[0:NV, 0:2, :].rearrange("p a n -> p (a n)")
        reachn1 = reach[0:NV, 2:4, :].rearrange("p a n -> p (a n)")
        s = {}

        def S(name):
            if name not in s:
                s[name] = sem(name)
            return s[name]

        for name in ("const_in", "weights_in", "wt_done", "wt_copied", "awd_done", "wa_done", "bias_done",
                     "x_in0", "x_in1", "adj_in0", "adj_in1", "mean_ready", "relu_done", "sd_ready", "turned",
                     "ht_ready", "hm_done", "row_ready", "row_out0", "row_out1", "sign_done", "packed",
                     "words_used", "dve", "init", "lists_done", "s2", "bmax_done", "s2pe", "sched_done",
                     "diffs", "diffs_used", "reach_ready", "fetched", "idx_ready", "z_ready", "prob_ready",
                     "y_ready", "summed", "flushed", "x_again", "out_ready", "out_done", "flag_done",
                     "passed", "drained", "flags_ready", "t4_adj", "t4_x", "t4_sign", "t4_packed",
                     "t4_count", "t4_most", "t4_steps_pe", "t4_steps_act", "t4_steps_pool", "t4_idx", "t4_rows", "t4_z", "t4_prob",
                     "t4_y", "t4_summed", "t4_out", "t4_stored", "g_in0", "g_in1", "g_in2", "g_in3", "pool"):
            S(name)

        block = ctx.enter_context(nc.Block())

        class Chain:

            def __init__(self, eng, name):
                self.eng, self.sem = eng, S(name)

            def step(self, ins):
                ins.then_inc(self.sem, 1)
                self.eng.wait_ge(self.sem, 1)
                self.eng.sem_inc(self.sem, -1)

        def take(eng, name, count=1):
            eng.wait_ge(S(name), count)
            eng.sem_inc(S(name), -count)

        class Landed:

            def __init__(self, eng, name, each):
                self.eng, self.name, self.each = eng, name, each
                self.reg = eng.alloc_register(f"{name}_{each}_count")
                eng.reg_mov(self.reg, 0)

            def wait(self):
                self.eng.reg_add(self.reg, self.reg, self.each)
                self.eng.wait_ge(S(self.name), self.eng.snap(self.reg)).then_inc(S("passed"), 1)

        def own_wait(eng, name, value):
            eng.wait_ge(S(name), value).then_inc(S("passed"), 1)

        @block.sync
        def _(sp):
            for k in const:
                sp.dma_start(C[k][:], const[k]).then_inc(S("const_in"), 16)
            sp.dma_start(wraw[:], W.rearrange("(c p) i -> p c i", p=P)).then_inc(S("weights_in"), 16)
            sp.dma_start(aw2[:], aw.rearrange("h d k -> (h d) k").rearrange("(c p) k -> p c k", p=P)).then_inc(S("weights_in"), 16)
            sp.dma_start(bcol[:], b.rearrange("(c p) -> p c", p=P), allow_slow_non_contiguous=True).then_inc(S("weights_in"), 16)
            sp.dma_start(bias[:], b.rearrange("(a n) -> a n", a=1).to_broadcast([P, D])).then_inc(S("weights_in"), 16)

            def store_row(t, par):
                sp.wait_ge(S("row_ready"), t + 1)
                sp.dma_start(table[bass.ds(t * P, P), :], trow[:, par, :]).then_inc(S(f"row_out{par}"), 16)

            def body(t, par, first):
                if not first:
                    sp.wait_ge(S("sign_done"), t - 1)
                sp.dma_start(aj[:, par, :], adj[bass.ds(t * P, P), :]).then_inc(S(f"adj_in{par}"), 16)
                if not first:
                    sp.wait_ge(S("relu_done"), t - 1)
                sp.dma_start(xt[:, par, :], x[bass.ds(t * P, P), :]).then_inc(S(f"x_in{par}"), 16)
                if not first:
                    store_row(t - 2, par)

            body(0, 0, True)
            body(1, 1, True)
            with sp.Fori(0, (NT - 2) // 2) as i:
                body(i * 2 + 2, 0, False)
                body(i * 2 + 3, 1, False)
            store_row(NT - 2, 0)
            store_row(NT - 1, 1)

            sp.dma_start(xo[:], x[0:P, :]).then_inc(S("x_again"), 16)
            with sp.Fori(0, NT - 1) as r:
                sp.wait_ge(S("out_ready"), r + 1)
                sp.dma_start(out[bass.ds(r * P, P), :], ob[:]).then_inc(S("out_done"), 16)
                sp.wait_ge(S("out_done"), r * 16 + 16)
                sp.dma_start(xo[:], x[bass.ds(r * P + P, P), :]).then_inc(S("x_again"), 16)
            sp.wait_ge(S("out_ready"), NT)
            sp.dma_start(out[(NT - 1) * P:NT * P, :], ob[:]).then_inc(S("out_done"), 16)
            sp.wait_ge(S("out_done"), 16 * NT)

            sp.wait_ge(S("drained"), 1)
            stored = Landed(sp, "t4_stored", 16)
            with sp.Fori(0, NT) as t:
                flagged = sp.value_load(missi[0:1, bass.ds(t, 1)], min_val=0, max_val=1)
                with sp.If(flagged > 0):
                    sp.dma_start(adj4, adj[bass.ds(t * P, P), :]).then_inc(S("t4_adj"), 16)
                    sp.dma_start(xo[:], x[bass.ds(t * P, P), :]).then_inc(S("t4_x"), 16)
                    take(sp, "t4_out")
                    sp.dma_start(out[bass.ds(t * P, P), :], ob[:]).then_inc(S("t4_stored"), 16)
                    stored.wait()

        @block.scalar
        def _(act):
            for c in range(KC):
                act.wait_ge(S("wt_done"), c + 1)
                nc.scalar.activation(wt[:, c, :], [psT, psH, psX, psY][c][:], ACT.Copy).then_inc(S("wt_copied"), 1)
            act.wait_ge(S("init"), 1)

            def body(t, par, k, first=False):
                act.wait_ge(S("mean_ready"), t + 1)
                if not first:
                    act.wait_ge(S("turned"), t)
                nc.scalar.activation(hn[:], xt[:, par, :], ACT.Relu, bias=negm[:, par:par + 1]).then_inc(S("relu_done"), 1)
                nc.scalar.activation(sd[:, par:par + 1], mv[:, par, 1:2], ACT.Sqrt, bias=epsc[:]).then_inc(S("sd_ready"), 1)
                act.wait_ge(S("turned"), t + 1)
                if not first:
                    act.wait_ge(S("hm_done"), t)
                nc.scalar.activation(ht[:].rearrange("p c n -> p (c n)"), psT[:], ACT.Copy).then_inc(S("ht_ready"), 1)
                act.wait_ge(S(f"adj_in{par}"), 16 * (k + 1) if isinstance(k, int) else k * 16 + 16)
                if not (isinstance(k, int) and k == 0):
                    act.wait_ge(S("packed"), t - 1)
                nc.scalar.activation(sg[:, par, :], aj[:, par, :], ACT.Sign, bias=halfc[:],
                                     accum_out=signsum[:, bass.ds(t, 1)]).then_inc(S("sign_done"), 1)

            body(0, 0, 0, True)
            body(1, 1, 0)
            with act.Fori(0, (NT - 2) // 2) as i:
                body(i * 2 + 2, 0, i + 1)
                body(i * 2 + 3, 1, i + 1)

            act.wait_ge(S("sched_done"), 1)
            q = act.value_load(iters[0:1, 0:1], min_val=1, max_val=QMAX)
            with act.Fori(0, q) as i:
                for u in range(RING):
                    act.wait_ge(S("z_ready"), i * RING + (u + 1))
                    nc.scalar.activation(prob[:, u, :, :], z[:], ACT.Exp).then_inc(S("prob_ready"), 1)

            act.wait_ge(S("flags_ready"), 1)
            adj_in = Landed(act, "t4_adj", 16)
            with act.Fori(0, NT) as t:
                flagged = act.value_load(missi[0:1, bass.ds(t, 1)], min_val=0, max_val=1)
                with act.If(flagged > 0):
                    adj_in.wait()
                    nc.scalar.activation(sign4, adj4, ACT.Sign, bias=halfc[:]).then_inc(S("t4_sign"), 1)
                    with act.Fori(0, NCH):
                        take(act, "t4_steps_act")
                        steps = act.value_load(steps4[0:1, 0:1], min_val=1, max_val=BITS * CW // 8)
                        with act.Fori(0, steps):
                            take(act, "t4_z")
                            nc.scalar.activation(prob8[:], z8[:], ACT.Exp).then_inc(S("t4_prob"), 1)

        @block.tensor
        def _(pe):
            pe.wait_ge(S("const_in"), 16 * len(const))
            pe.wait_ge(S("weights_in"), 64)
            for c in range(KC):
                dst = [psT, psH, psX, psY][c]
                for o in range(KC):
                    last = nc.tensor.transpose(dst[:, o * P:(o + 1) * P], wraw[:, o, c * P:(c + 1) * P], eye[:])
                last.then_inc(S("wt_done"), 1)
            pe.wait_ge(S("awd_done"), 1)
            for c in range(KC):
                for o in range(KC):
                    nc.tensor.matmul(psA[:, c * 16:c * 16 + 16], wraw[:, o, c * P:(c + 1) * P], awd[:, o, :],
                                     start=(o == 0), stop=(o == KC - 1))
            for o in range(KC):
                last = nc.tensor.matmul(psA[:, 64:80], biasrep[:, o, :], awd[:, o, :], start=(o == 0), stop=(o == KC - 1))
            last.then_inc(S("wa_done"), 1)
            pe.wait_ge(S("bias_done"), 1)
            pe.wait_ge(S("wt_copied"), KC)

            def pack(signs):
                for lo, n in ((0, 512), (512, 256)):
                    for k in range(BITS):
                        nc.tensor.matmul(psW[:, lo:lo + n], packs[:, k, :],
                                         signs[:, k * NW + lo:k * NW + lo + n], start=(k == 0), stop=False)
                    last = nc.tensor.matmul(psW[:, lo:lo + n], ones2[:], wordrow[:, lo:lo + n],
                                            start=False, stop=True)
                return last

            def body(t, par, first=False):
                pe.wait_ge(S("relu_done"), t + 1)
                if not first:
                    pe.wait_ge(S("ht_ready"), t)
                for c in range(KC):
                    last = nc.tensor.transpose(psT[:, c * P:(c + 1) * P], hn[:, c * P:(c + 1) * P], eye[:])
                last.then_inc(S("turned"), 1)
                pe.wait_ge(S("ht_ready"), t + 1)
                if not first:
                    pe.wait_ge(S("row_ready"), t)
                for c in range(KC):
                    nc.tensor.matmul(psH[:], ht[:, c, :], wt[:, c, :], start=(c == 0), stop=(c == KC - 1))
                for c in range(KC):
                    last = nc.tensor.matmul(psS[:, 0:16], ht[:, c, :], wa[:, c, :], start=(c == 0), stop=(c == KC - 1))
                last.then_inc(S("hm_done"), 1)
                pe.wait_ge(S("sign_done"), t + 1)
                if not first:
                    pe.wait_ge(S("words_used"), t)
                pack(sg[:, par, :]).then_inc(S("packed"), 1)

            body(0, 0, True)
            body(1, 1)
            with pe.Fori(0, (NT - 2) // 2) as i:
                body(i * 2 + 2, 0)
                body(i * 2 + 3, 1)

            pe.wait_ge(S("s2"), 1)
            nc.tensor.matmul(psT[:, 0:NV], C["before"][:], cnt[:], start=True, stop=True)
            nc.tensor.matmul(psH[0:NV, 0:1], cnt[:], C["ones"][:, 0:1], start=True, stop=True).then_inc(S("s2pe"), 1)
            pe.wait_ge(S("s2"), 2)
            nc.tensor.matmul(psX[0:NV, 0:1], C["upto"][0:NV, 0:NV], nb[:], start=True, stop=True)
            nc.tensor.matmul(psY[0:1, 0:1], nb[:], C["ones"][0:NV, 0:1], start=True, stop=True).then_inc(S("s2pe"), 1)
            for g in range(8):
                pe.wait_ge(S("s2"), 3)
                if g >= 2:
                    pe.wait_ge(S("diffs_used"), g - 1)
                nc.tensor.matmul([psA, psD][g % 2][:, 0:7 * VC], C["diff"][:],
                                 V[:, 7 * g:7 * g + 7, :].rearrange("p v c -> p (v c)"),
                                 start=True, stop=True).then_inc(S("diffs"), 1)
            pe.wait_ge(S("diffs_used"), 7)
            nc.tensor.matmul(psA[:, 0:7 * VC], C["diff"][:], V[:, 56:63, :].rearrange("p v c -> p (v c)"),
                             start=True, stop=True).then_inc(S("diffs"), 1)
            for j in range(NMAX // 512):
                pe.wait_ge(S("s2"), 4 + j)
                nc.tensor.matmul(psT[0:1, :], C["ones"][0:NV, 0:1], reachn, start=True, stop=True)
                nc.tensor.matmul(psH[0:1, :], nb[:], reachn, start=True, stop=True)
                nc.tensor.matmul(psX[0:1, :], C["newrow"][:], reachn, start=True, stop=True)
                nc.tensor.matmul(psY[0:1, :], C["newrow"][:], reachn1, start=True, stop=True).then_inc(S("s2pe"), 1)
            pe.wait_ge(S("sched_done"), 1)
            q = pe.value_load(iters[0:1, 0:1], min_val=1, max_val=QMAX)

            def fetch(n, u):
                own_wait(pe, "reach_ready", n + 1)
                v = pe.value_load(sched[0:1, 0, bass.ds(n, 1)], min_val=0, max_val=NV)
                for g in range(2):
                    last = nc.tensor.matmul(fetchd[u][:, g * VC:(g + 1) * VC], reach[:, u, g * P:(g + 1) * P],
                                            Dv[:, bass.ds(v, 1), :].rearrange("p v c -> p (v c)"), start=True, stop=True)
                last.then_inc(S("fetched"), 1)

            def clear(counted=False):
                a = nc.tensor.matmul(psA[:], zero[:], zrow[:], start=True, stop=False, skip_group_check=True)
                d = nc.tensor.matmul(psD[:, 0:H], zero[:], zrow[:, 0:H], start=True, stop=False, skip_group_check=True)
                if counted:
                    a.then_inc(S("summed"), 1)
                    d.then_inc(S("summed"), 1)
                return d

            for m in range(LAG + 1):
                fetch(m, m)
            clear(True)
            with pe.Fori(0, q) as i:
                for u in range(RING):
                    n = i * RING + u
                    fetch(n + (LAG + 1), (u + LAG + 1) % RING)
                    pe.wait_ge(S("y_ready"), n + 1)
                    for g in range(2):
                        nc.tensor.matmul(psA[:], sel[:, u, g, :], Y[:, 2 * u + g, :], start=False, stop=False,
                                         skip_group_check=True)
                        last = nc.tensor.matmul(psD[:, 0:H], sel[:, u, g, :], prob[:, u, g, :], start=False, stop=False,
                                                skip_group_check=True)
                    last.then_inc(S("summed"), 1)
                    ends = pe.value_load(sched[0:1, 2, bass.ds(n, 1)], min_val=0, max_val=1)
                    r = pe.value_load(sched[0:1, 3, bass.ds(n, 1)], min_val=0, max_val=NT)
                    with pe.If(ends > 0):
                        pe.wait_ge(S("flushed"), r + 1)
                        clear()

            pe.wait_ge(S("flags_ready"), 1)
            with pe.Fori(0, NT) as t:
                flagged = pe.value_load(missi[0:1, bass.ds(t, 1)], min_val=0, max_val=1)
                with pe.If(flagged > 0):
                    take(pe, "t4_sign")
                    pack(sign4)
                    clear().then_inc(S("t4_packed"), 1)
                    with pe.Fori(0, NCH):
                        take(pe, "t4_steps_pe")
                        steps = pe.value_load(steps4[0:1, 0:1], min_val=1, max_val=BITS * CW // 8)
                        with pe.Fori(0, steps):
                            take(pe, "t4_y")
                            for g in range(8):
                                nc.tensor.matmul(psA[:], eye[:], G4[:, g, 0:D], start=False, stop=False,
                                                 skip_group_check=True)
                                last = nc.tensor.matmul(psD[:, 0:H], eye[:], prob8[:, g, :], start=False, stop=False,
                                                        skip_group_check=True)
                            last.then_inc(S("t4_summed"), 1)

        @block.vector
        def _(dve):
            ch = Chain(dve, "dve")
            v_ = nc.vector
            v_.memset(epsc[:], 1e-5)
            v_.memset(halfc[:], -0.5)
            v_.memset(V[:], 0.0)
            v_.memset(lst[:], 0.0)
            v_.memset(zero[:], 0.0)
            v_.memset(zrow[:], 0.0)
            v_.memset(starts[:, NV:NVP], 0.0)
            ch.step(v_.memset(awd[:], 0.0))
            dve.wait_ge(S("const_in"), 16 * len(const))
            dve.wait_ge(S("weights_in"), 64)
            for k in range(BITS):
                v_.tensor_scalar(packs[:, k, :], eye[:], float(WSC * 2 ** k), None, ALU.mult)
            v_.memset(ones2[:], 1.0)
            v_.tensor_copy(wordrow[:], C["wordrow"][:])
            v_.memset(cnt0[:], 0.0).then_inc(S("init"), 1)
            for o in range(KC):
                for half in range(2):
                    h = 2 * o + half
                    rows = slice(half * DH, (half + 1) * DH)
                    v_.tensor_copy(awd[rows, o, h:h + 1], aw2[rows, o, 0:1])
                    v_.tensor_copy(awd[rows, o, H + h:H + h + 1], aw2[rows, o, 1:2])
            v_.tensor_copy(biasrep[:], bcol[:].unsqueeze(2).to_broadcast([P, KC, P])).then_inc(S("awd_done"), 1)
            dve.wait_ge(S("wa_done"), 1)
            v_.tensor_copy(wa[:].rearrange("p c k -> p (c k)"), psA[:, 0:64])
            v_.tensor_copy(abias[:], psA[:, 64:80]).then_inc(S("bias_done"), 1)
            dve.wait_ge(S("bias_done"), 1)

            def mean(t, par, k):
                dve.wait_ge(S(f"x_in{par}"), 16 * (k + 1) if isinstance(k, int) else k * 16 + 16)
                ch.step(v_.bn_stats(stats[:, par, :], xt[:, par, :]))
                if not (isinstance(t, int) and t < 2):
                    own_wait(dve, "sd_ready", t - 1)
                ch.step(v_.bn_aggr(mv[:, par, :], stats[:, par, :]))
                v_.tensor_scalar(negm[:, par:par + 1], mv[:, par, 0:1], -1.0, None, ALU.mult).then_inc(S("mean_ready"), 1)

            def rows(t, par, k):
                own_wait(dve, "sd_ready", t + 1)
                ch.step(v_.reciprocal(rs[:, par:par + 1], sd[:, par:par + 1]))
                dve.wait_ge(S("hm_done"), t + 1)
                if k is not None:
                    dve.wait_ge(S(f"row_out{par}"), k * 16)
                v_.scalar_tensor_tensor(ab[:, bass.ds(t, 1), :].rearrange("p a c -> p (a c)"), psS[:, 0:16],
                                        rs[:, par:par + 1], abias[:], ALU.mult, ALU.add)
                v_.scalar_tensor_tensor(trow[:, par, D:TR], psS[:, H:2 * H],
                                        rs[:, par:par + 1], abias[:, H:2 * H], ALU.mult, ALU.add)
                v_.scalar_tensor_tensor(trow[:, par, 0:D], psH[:], rs[:, par:par + 1], bias[:],
                                        ALU.mult, ALU.add).then_inc(S("row_ready"), 1)

            def candidates(src, nw):
                first = v_.tensor_scalar(wint[:, 0:nw], src, float(WSC * 255), None, ALU.add)
                ch.step(first)
                v_.tensor_tensor(bits[:, :, 0:nw], wint[:, 0:nw].unsqueeze(1).to_broadcast([P, BITS, nw]),
                                 C["bitmask"][:].unsqueeze(2).to_broadcast([P, BITS, nw]), ALU.bitwise_and)
                ch.step(v_.tensor_scalar(widx[:, 0:nw], wint[:, 0:nw], 2 * WSC - 1, None, ALU.bitwise_and))
                ch.step(v_.tensor_scalar(wneg[:, 0:nw], widx[:, 0:nw], -1.0, float(TOP), ALU.mult, ALU.add))
                ch.step(v_.tensor_tensor(cand[:, :, 0:nw], wneg[:, 0:nw].unsqueeze(1).to_broadcast([P, BITS, nw]),
                                         C["bitcol"][:].unsqueeze(2).to_broadcast([P, BITS, nw]), ALU.subtract))
                ch.step(v_.scalar_tensor_tensor(cand[:, :, 0:nw], bits[:, :, 0:nw], 0.0, cand[:, :, 0:nw],
                                                ALU.is_gt, ALU.mult))

            def expand(src, nw, nl, dst_v):
                candidates(src, nw)
                for r in range(nl):
                    ch.step(v_.max(lst[:, 8 * r:8 * r + 8], cand[:, :, 0:nw]))
                    if r < nl - 1:
                        ch.step(v_.match_replace(cand[:, :, 0:nw], lst[:, 8 * r:8 * r + 8], cand[:, :, 0:nw], 0.0))
                ch.step(v_.tensor_copy(V[:, bass.ds(dst_v, 1), 18:18 + 8 * nl].rearrange("p a c -> p (a c)"), lst[:, 0:8 * nl]))

            def lists(t):
                own_wait(dve, "packed", t + 1)
                for c in range(NCH):
                    last = v_.max(tops[:, 8 * c:8 * c + 8], psW[:, CW * c:CW * c + CW])
                last.then_inc(S("words_used"), 1)
                own_wait(dve, "words_used", t + 1)
                for r in range(LW // 8):
                    ch.step(v_.max(wl[:, 8 * r:8 * r + 8], tops[:]))
                    if r < LW // 8 - 1:
                        ch.step(v_.match_replace(tops[:], wl[:, 8 * r:8 * r + 8], tops[:], GONE))
                expand(wl[:], LW, LW // 8, t + (NCH - 1))

            mean(0, 0, 0)
            mean(1, 1, 0)
            rows(0, 0, None)
            dve.wait_ge(S("packed"), 1)
            with dve.Fori(0, NCH) as c:
                expand(psW[:, bass.ds(c * CW, CW)], CW, K // 8, c)
            v_.tensor_copy(cnt0[:], psW[:, 0:1]).then_inc(S("words_used"), 1)
            mean(2, 0, 1)
            rows(1, 1, None)
            lists(1)
            with dve.Fori(0, (NT - 4) // 2) as i:
                for par in range(2):
                    t = i * 2 + (2 + par)
                    mean(t + 1, 1 - par, i + 1 + par)
                    rows(t, par, i + 1)
                    lists(t)
            mean(NT - 1, 1, NT // 2 - 1)
            rows(NT - 2, 0, NT // 2 - 1)
            lists(NT - 2)
            rows(NT - 1, 1, NT // 2 - 1)
            lists(NT - 1)

            ch.step(v_.tensor_reduce(bmax1[:], ab[:, :, H:2 * H].rearrange("p t h -> p h t"), AX.X, ALU.max))
            dve.wait_ge(S("sign_done"), NT)
            ch.step(v_.memset(G[:, :, :], 0.0))
            v_.memset(G[:, :, D:TR], FAR)
            dve.wait_ge(S("packed"), NT)
            v_.memset(Dv[:, NV, :], 0.0)
            ones4 = aj[:, 1, 0:NV * K].bitcast(f32).rearrange("p (v k) -> p v k", k=K)
            ch.step(v_.tensor_scalar(ones4, V[:, 0:NV, 18:VC], 0.0, None, ALU.is_gt))
            v_.tensor_reduce(cnt[:], ones4, AX.X, ALU.add).then_inc(S("s2"), 1)
            dve.wait_ge(S("s2"), 1)
            ch.step(v_.tensor_reduce(cnt0[:], cnt[:, 0:NCH], AX.X, ALU.add))
            ch.step(v_.tensor_scalar(miss[:], signsum[:], 0.5, float(N // 2), ALU.mult, ALU.add))
            v_.tensor_tensor(miss[:, 0:1], miss[:, 0:1], cnt0[:], ALU.subtract)
            ch.step(v_.tensor_tensor(miss[:, 1:NT], miss[:, 1:NT], cnt[:, NCH:NV], ALU.subtract))
            v_.tensor_copy(cnt0[:], cnt0[:]).then_inc(S("lists_done"), 1)
            dve.wait_ge(S("s2pe"), 1)
            ch.step(v_.tensor_scalar(nbi[:], psH[0:NV, 0:1], float(PE_ - 1), None, ALU.add))
            ch.step(v_.tensor_scalar(nbi[:], nbi[:], 8, None, ALU.arith_shift_right))
            ch.step(v_.tensor_copy(nb[:], nbi[:]))
            v_.tensor_tensor(nb[:], nb[:], C["newrow"][:], ALU.max).then_inc(S("s2"), 1)
            ch.step(v_.tensor_copy(starts[:, 0:NV], psT[:, 0:NV]))
            v_.tensor_copy(V[:, 0:NV, 0:1].rearrange("p v c -> p (v c)"), starts[:, 0:NV])
            v_.tensor_copy(V[:, 0:NV, 1:2].rearrange("p v c -> p (v c)"), C["row"][:].to_broadcast([P, NV]))
            v_.tensor_copy(V[:, 0:NCH, 2:2 + H], ab[:, 0:1, 0:H].to_broadcast([P, NCH, H]))
            v_.tensor_copy(V[:, NCH:NV, 2:2 + H], ab[:, 1:NT, 0:H])
            dve.wait_ge(S("bmax_done"), 1)
            ch.step(v_.tensor_tensor(bound[:], ab[:, :, 0:H], bmax[:].unsqueeze(1).to_broadcast([P, NT, H]), ALU.add))
            ch.step(v_.scalar_tensor_tensor(bound[:], bound[:], ALPHA, bound[:], ALU.mult, ALU.max))
            ch.step(v_.tensor_scalar(bound[:], bound[:], -HEADROOM, None, ALU.add))
            v_.tensor_copy(V[:, 0:NCH, 2 + H:2 + 2 * H], bound[:, 0:1, :].to_broadcast([P, NCH, H]))
            v_.tensor_copy(V[:, NCH:NV, 2 + H:2 + 2 * H], bound[:, 1:NT, :]).then_inc(S("s2"), 1)
            dve.wait_ge(S("s2pe"), 2)
            ch.step(v_.tensor_copy(cum[:], psX[0:NV, 0:1]))
            ch.step(v_.tensor_scalar(iters[:], psY[0:1, 0:1], float(RING - 1), None, ALU.add))
            ch.step(v_.tensor_scalar(iters[:], iters[:], RING.bit_length() - 1, None, ALU.arith_shift_right))
            for g in range(9):
                dve.wait_ge(S("diffs"), g + 1)
                v_.tensor_copy(Dv[:, 7 * g:7 * g + 7, :].rearrange("p v c -> p (v c)"),
                               [psA, psD][g % 2][:, 0:7 * VC]).then_inc(S("diffs_used"), 1)
            for j in range(NMAX // 512):
                if j:
                    dve.wait_ge(S("s2pe"), 2 + j)
                v_.tensor_scalar(reachn, C["steps"][:, j * 512:j * 512 + 512], cum[:], None, ALU.is_ge)
                v_.tensor_scalar(reachn1, C["steps"][:, j * 512 + 1:j * 512 + 513], cum[:], None,
                                 ALU.is_ge).then_inc(S("s2"), 1)
                dve.wait_ge(S("s2pe"), 3 + j)
                cols = slice(j * 512, j * 512 + 512)
                v_.tensor_copy(sched[0:1, 0, cols], psT[0:1, :])
                ch.step(v_.tensor_copy(vrow[:], psX[0:1, :]))
                v_.tensor_tensor(sched[0:1, 2, cols], psY[0:1, :], vrow[:], ALU.subtract)
                ch.step(v_.tensor_copy(sched[0:1, 3, cols], vrow[:]))
                ch.step(v_.tensor_tensor(sched[0:1, 1, cols], C["steps"][0:1, cols], psH[0:1, :], ALU.subtract))
            v_.tensor_copy(cnt0[:], cnt0[:]).then_inc(S("sched_done"), 1)
            dve.wait_ge(S("sched_done"), 1)

            q = dve.value_load(iters[0:1, 0:1], min_val=1, max_val=QMAX)

            def reach_of(n, u):
                v = dve.value_load(sched[0:1, 0, bass.ds(n, 1)], min_val=0, max_val=NV)
                bb = dve.value_load(sched[0:1, 1, bass.ds(n, 1)], min_val=0, max_val=NB - 1)
                v_.tensor_scalar(reach[:, u, :], C["count"][:], C["batchbase"][:, bass.ds(bb, 1)],
                                 starts[:, bass.ds(v, 1)], ALU.add, ALU.is_ge).then_inc(S("reach_ready"), 1)

            def choose(n, u):
                own_wait(dve, "fetched", n + 1)
                F = fetchd[u][:, 0:2 * VC].rearrange("p (g c) -> p g c", g=2)
                bb = dve.value_load(sched[0:1, 1, bass.ds(n, 1)], min_val=0, max_val=NB - 1)
                ch.step(v_.tensor_tensor(rank[:], C["flatpos"][:, bass.ds(bb * 2, 2)], F[:, :, 0], ALU.subtract))
                ch.step(v_.tensor_tensor(hit[:], C["count"][:, 0:K].unsqueeze(1).to_broadcast([P, 2, K]),
                                         rank[:].unsqueeze(2).to_broadcast([P, 2, K]), ALU.is_equal))
                ch.step(v_.tensor_tensor(pick[:], hit[:], F[:, :, 18:VC], ALU.mult))
                ch.step(v_.tensor_reduce(val[:], pick[:], AX.X, ALU.add))
                if not isinstance(n, int):
                    own_wait(dve, "summed", n + (2 - RING + 1))
                v_.tensor_scalar(idx[:, u, :], val[:], -1.0, float(TOP), ALU.mult, ALU.add).then_inc(S("idx_ready"), 1)
                ch.step(v_.tensor_scalar(live[:], val[:], 0.0, None, ALU.is_gt))
                for g in range(2):
                    last = v_.tensor_scalar(sel[:, u, g, :], C["count"][:, 0:P], F[:, g, 1:2], live[:, g:g + 1],
                                            ALU.is_equal, ALU.mult)

            def scores(n, u, gathers):
                dve.wait_ge(S(f"g_in{u}"), gathers)
                F = fetchd[u][:, 0:2 * VC].rearrange("p (g c) -> p g c", g=2)
                ch.step(v_.tensor_tensor(z2[:], G[:, 2 * u:2 * u + 2, D:TR], F[:, :, 2:2 + H], ALU.add))
                ch.step(v_.scalar_tensor_tensor(z2[:], z2[:], ALPHA, z2[:], ALU.mult, ALU.max))
                v_.tensor_tensor(z[:], z2[:], F[:, :, 2 + H:2 + 2 * H], ALU.subtract).then_inc(S("z_ready"), 1)

            def weigh(n, u):
                dve.wait_ge(S("prob_ready"), n + 1)
                g = G[:, 2 * u:2 * u + 2, 0:D].rearrange("p g (h d) -> p g h d", h=H)
                y = Y[:, 2 * u:2 * u + 2, :].rearrange("p g (h d) -> p g h d", h=H)
                v_.tensor_tensor(y, g, prob[:, u, :, :].unsqueeze(3).to_broadcast([P, 2, H, DH]),
                                 ALU.mult).then_inc(S("y_ready"), 1)

            def flush(n):
                own_wait(dve, "summed", n + 3)
                r = dve.value_load(sched[0:1, 3, bass.ds(n, 1)], min_val=0, max_val=NT - 1)
                v_.tensor_scalar(den[:], psD[:, 0:H], 1e-37, None, ALU.max).then_inc(S("flag_done"), 1)
                dve.wait_ge(S("flag_done"), r * 3 + 1)
                v_.reciprocal(rden[:], den[:]).then_inc(S("flag_done"), 1)
                dve.wait_ge(S("flag_done"), r * 3 + 2)
                dve.wait_ge(S("x_again"), r * 16 + 16)
                v_.tensor_tensor(ob[:].rearrange("p (h d) -> p h d", h=H), psA[:].rearrange("p (h d) -> p h d", h=H),
                                 rden[:].unsqueeze(2).to_broadcast([P, H, DH]), ALU.mult).then_inc(S("flag_done"), 1)
                dve.wait_ge(S("flag_done"), r * 3 + 3)
                v_.tensor_copy(den[:], den[:]).then_inc(S("flushed"), 1)
                v_.tensor_tensor(ob[:], ob[:], xo[:], ALU.add).then_inc(S("out_ready"), 1)

            for m in range(LAG + 1):
                reach_of(m, m)
            for m in range(LAG):
                choose(m, m)
            with dve.Fori(0, q) as i:
                for u in range(RING):
                    n = i * RING + u
                    scores(n, u, i * 32 + 32)
                    reach_of(n + (LAG + 1), (u + LAG + 1) % RING)
                    choose(n + LAG, (u + LAG) % RING)
                    weigh(n, u)
                    ends = dve.value_load(sched[0:1, 2, bass.ds(n, 1)], min_val=0, max_val=1)
                    with dve.If(ends > 0):
                        flush(n)

            dve.wait_ge(S("flags_ready"), 1)
            dve.wait_ge(S("drained"), 1)
            own_wait(dve, "summed", q * RING + 2)
            rows_in = Landed(dve, "t4_rows", 8 * 16)
            x_in = Landed(dve, "t4_x", 16)
            ch.step(v_.memset(G4[:], 0.0))
            with dve.Fori(0, NT) as t:
                flagged = dve.value_load(missi[0:1, bass.ds(t, 1)], min_val=0, max_val=1)
                with dve.If(flagged > 0):
                    take(dve, "t4_packed")
                    with dve.Fori(0, NCH) as c:
                        candidates(psW[:, bass.ds(c * CW, CW)], CW)
                        ch.step(v_.tensor_scalar(bits[:], cand[:], 0.0, None, ALU.is_gt))
                        v_.tensor_reduce(count4[:], bits[:].rearrange("p k w -> p (k w)"), AX.X,
                                         ALU.add).then_inc(S("t4_count"), 1)
                        take(dve, "t4_most")
                        ch.step(v_.tensor_scalar(steps4[:], most[0:1, :], 1.0, 7.0, ALU.max, ALU.add))
                        ch.step(v_.tensor_scalar(steps4[:], steps4[:], 3, None, ALU.arith_shift_right))
                        for name in ("t4_steps_pe", "t4_steps_act", "t4_steps_pool"):
                            dve.sem_inc(S(name), 1)
                        steps = dve.value_load(steps4[0:1, 0:1], min_val=1, max_val=BITS * CW // 8)
                        with dve.Fori(0, steps):
                            ch.step(v_.max(l8[:], cand[:]))
                            v_.tensor_scalar(pen8[:], l8[:], 0.0, FAR, ALU.is_equal, ALU.mult)
                            v_.tensor_scalar(idx8[:], l8[:], -1.0, float(TOP), ALU.mult, ALU.add).then_inc(S("t4_idx"), 1)
                            ch.step(v_.match_replace(cand[:], l8[:], cand[:], 0.0))
                            rows_in.wait()
                            ch.step(v_.tensor_tensor(z8[:], G4[:, :, D:TR], ab[:, bass.ds(t, 1), 0:H].to_broadcast([P, 8, H]), ALU.add))
                            ch.step(v_.scalar_tensor_tensor(z8[:], z8[:], ALPHA, z8[:], ALU.mult, ALU.max))
                            ch.step(v_.tensor_tensor(z8[:], z8[:], bound[:, bass.ds(t, 1), :].to_broadcast([P, 8, H]), ALU.subtract))
                            v_.tensor_tensor(z8[:], z8[:], pen8[:].unsqueeze(2).to_broadcast([P, 8, H]),
                                             ALU.add).then_inc(S("t4_z"), 1)
                            take(dve, "t4_prob")
                            for g in range(8):
                                y = G4[:, g, 0:D].rearrange("p (h d) -> p h d", h=H)
                                last = v_.tensor_tensor(y, y, prob8[:, g, :].unsqueeze(2).to_broadcast([P, H, DH]), ALU.mult)
                            last.then_inc(S("t4_y"), 1)
                            take(dve, "t4_summed")
                    ch.step(v_.tensor_scalar(den[:], psD[:, 0:H], 1e-37, None, ALU.max))
                    ch.step(v_.reciprocal(rden[:], den[:]))
                    x_in.wait()
                    ch.step(v_.tensor_tensor(ob[:].rearrange("p (h d) -> p h d", h=H), psA[:].rearrange("p (h d) -> p h d", h=H),
                                             rden[:].unsqueeze(2).to_broadcast([P, H, DH]), ALU.mult))
                    v_.tensor_tensor(ob[:], ob[:], xo[:], ALU.add).then_inc(S("t4_out"), 1)

        @block.gpsimd
        def _(pool):
            pool.wait_ge(S("lists_done"), 1)
            nc.gpsimd.partition_all_reduce(bmax[:], bmax1[:], P, bass.bass_isa.ReduceOp.max).then_inc(S("bmax_done"), 1)
            nc.gpsimd.partition_all_reduce(missmax[:], miss[:], P, bass.bass_isa.ReduceOp.max).then_inc(S("pool"), 1)
            pool.wait_ge(S("pool"), 1)
            nc.gpsimd.tensor_scalar(missi[:], missmax[:], 0.0, None, ALU.is_gt).then_inc(S("flags_ready"), 1)
            pool.wait_ge(S("flags_ready"), 1)
            for par in range(2):
                pool.wait_ge(S(f"row_out{par}"), 16 * NT // 2)
            pool.wait_ge(S("sched_done"), 1)
            q = pool.value_load(iters[0:1, 0:1], min_val=1, max_val=QMAX)

            def gather(n, u):
                own_wait(pool, "idx_ready", n + 1)
                for g in range(2):
                    nc.gpsimd.indirect_dma_start(
                        out=G[:, 2 * u + g, :], out_offset=None, in_=table,
                        in_offset=bass.IndirectOffsetOnAxis(ap=idx[:, u, g:g + 1], axis=0),
                        bounds_check=N - 1, oob_is_err=False).then_inc(S(f"g_in{u}"), 16)

            for m in range(LAG):
                gather(m, m)
            with pool.Fori(0, q) as i:
                for u in range(RING):
                    gather(i * RING + (u + LAG), (u + LAG) % RING)
            for m in range(LAG):
                own_wait(pool, f"g_in{m}", q * 32 + 32)

            pool.sem_inc(S("drained"), 1)

            with pool.Fori(0, NT) as t:
                flagged = pool.value_load(missi[0:1, bass.ds(t, 1)], min_val=0, max_val=1)
                with pool.If(flagged > 0):
                    with pool.Fori(0, NCH):
                        take(pool, "t4_count")
                        nc.gpsimd.partition_all_reduce(most[:], count4[:], P, bass.bass_isa.ReduceOp.max).then_inc(S("t4_most"), 1)
                        take(pool, "t4_steps_pool")
                        steps = pool.value_load(steps4[0:1, 0:1], min_val=1, max_val=BITS * CW // 8)
                        with pool.Fori(0, steps):
                            take(pool, "t4_idx")
                            for g in range(8):
                                nc.gpsimd.indirect_dma_start(
                                    out=G4[:, g, :], out_offset=None, in_=table,
                                    in_offset=bass.IndirectOffsetOnAxis(ap=idx8[:, g:g + 1], axis=0),
                                    bounds_check=N - 1, oob_is_err=False).then_inc(S("t4_rows"), 16)


_INS = ["x", "adj", "L0_gnn_W", "L0_gnn_b", "L0_gnn_aw"]
_OUTS = [((N, D), "float32")]


def kernel(**inputs):
    import numpy as _np
    import concourse.bacc as _bacc
    from concourse import mybir as _mybir
    from concourse.bass_utils import run_bass_kernel_spmd as _run

    nc = _bacc.Bacc("TRN2", target_bir_lowering=False, num_devices=1)
    arrays, args, const = {}, [], {}
    for name in _INS:
        a = _np.ascontiguousarray(inputs[name])
        arrays[f"in_{name}_dram"] = a
        args.append(nc.dram_tensor(f"in_{name}_dram", a.shape, _mybir.dt.from_np(a.dtype), kind="ExternalInput").ap())
    for name, a in constants().items():
        arrays[f"const_{name}_dram"] = a
        const[name] = nc.dram_tensor(f"const_{name}_dram", a.shape, _mybir.dt.from_np(a.dtype), kind="ExternalInput").ap()
    outs = []
    for i, (shape, dtype) in enumerate(_OUTS):
        dt = _mybir.dt.from_np(_np.dtype(dtype))
        outs.append(nc.dram_tensor(f"out_{i}_dram", shape, dt, kind="ExternalOutput").ap())
    build(nc, *args, const, *outs)
    r = _run(nc, [arrays], core_ids=[0])
    got = tuple(r.results[0][f"out_{i}_dram"] for i in range(len(_OUTS)))
    return got[0]
```

```python
import concourse.bass as bass
from concourse import mybir
from contextlib import ExitStack


N, D, H, DH = 6144, 512, 8, 64
P = 128
NT = N // P
KC = D // P
BITS = 8
NW = N // BITS
NCH = 16
CW = NW // NCH
LW = 40
K = 48
TOP = N
WSC = 1024
NV = NCH + NT - 1
NVP = NV + 1
VC = 2 + 2 * H + K
HALF = D // 2 + H // 2
TR = 2 * HALF
GS = 4
SW = 448
NMAX = 6 * SW
LAG = 2
RING = 4
CLEARED = (RING - 1) * GS
QMAX = -(-(NCH * K + (NT - 1) * LW) // (GS * RING))
ALPHA = 0.2
HEADROOM = 40.0
GONE = -3.0e5
FAR = -1.0e30


def constants():
    import numpy as np

    f = np.float32
    eye = np.eye(P, dtype=f)
    c = {}
    c["eye"] = eye
    w = np.arange(NW)
    c["wordrow"] = np.stack([w // 256 * 256, w % 256]).astype(f)
    c["bitmask"] = np.tile((1 << (11 + np.arange(BITS))).astype(np.int32), (P, 1))
    c["bitcol"] = np.tile((NW * np.arange(BITS)).astype(f), (P, 1))
    c["count"] = np.tile(np.arange(SW + 1).astype(f), (P, 1))
    c["before"] = (np.arange(P)[:, None] < np.arange(P)[None, :]).astype(f)
    c["diff"] = eye - np.eye(P, k=1, dtype=f)
    c["upto"] = (np.arange(P)[:, None] <= np.arange(P)[None, :]).astype(f)
    c["row1"] = np.arange(1, P + 1, dtype=f)[:, None].copy()
    c["rankoff"] = (np.arange(K)[None, :] - np.arange(P)[:, None]).astype(f)
    v = np.arange(NV)
    c["newrow"] = (v >= NCH - 1).astype(f)[:, None].copy()
    c["ones"] = np.ones((P, P), f)
    return c


def build(nc, x, adj, W, b, aw, const, out):
    f32, bf16, i32 = mybir.dt.float32, mybir.dt.bfloat16, mybir.dt.int32
    ALU, ACT, AX = mybir.AluOpType, mybir.ActivationFunctionType, mybir.AxisListType
    table = nc.dram_tensor("table", [TOP + 1, TR], f32).ap()

    ctx = ExitStack()
    with ctx:
        def sb(name, shape, dt):
            return ctx.enter_context(nc.sbuf_tensor(name, shape, dt))

        def pb(name, shape):
            return ctx.enter_context(nc.psum_tensor(name, shape, f32))

        def sem(name):
            return ctx.enter_context(nc.semaphore(name))

        C = {k: sb("c_" + k, list(const[k].shape), const[k].dtype) for k in const}
        eye = C["eye"]
        packs = sb("packs", [P, BITS, P], bf16)
        wordrow = sb("wordrow", [2, NW], bf16)
        ones2 = sb("ones2", [2, P], bf16)

        xt = sb("xt", [P, 2, D], f32)
        hn = sb("hn", [P, D], f32)
        ht = sb("ht", [P, KC, P], f32)
        wraw = sb("wraw", [P, KC, D], f32)
        wt = sb("wt", [P, KC, D], f32)
        aw2 = sb("aw2", [P, KC, 2], f32)
        awd = sb("awd", [P, KC, 2 * H], f32)
        wa = sb("wa", [P, KC, 2 * H], f32)
        bcol = sb("bcol", [P, KC], f32)
        bias = sb("bias", [P, D], f32)
        biasrep = sb("biasrep", [P, KC, P], f32)
        abias = sb("abias", [P, 2 * H], f32)
        stats = sb("stats", [P, 2, 6], f32)
        mv = sb("mv", [P, 2, 2], f32)
        negm = sb("negm", [P, 2], f32)
        sd = sb("sd", [P, 2], f32)
        rs = sb("rs", [P, 2], f32)
        epsc = sb("epsc", [P, 1], f32)
        halfc = sb("halfc", [P, 1], f32)
        trow = sb("trow", [P, 2, TR], f32)
        ab = sb("ab", [P, NT, 2 * H], f32)
        aj = sb("aj", [P, 2, N], i32)
        sg = sb("sg", [P, 2, N], bf16)
        signsum = sb("signsum", [P, NT], f32)
        tops = sb("tops", [P, NCH * 8], f32)
        wl = sb("wl", [P, LW], f32)
        wint = sb("wint", [P, CW], i32)
        widx = sb("widx", [P, CW], i32)
        wneg = sb("wneg", [P, CW], f32)
        bits = sb("bits", [P, BITS, CW], i32)
        cand = sb("cand", [P, BITS, CW], f32)
        lst = sb("lst", [P, K], f32)
        V = sb("V", [P, NVP, VC], f32)
        Dv = sg[:, 0:2, :].rearrange("p a n -> p (a n)")[:, 0:2 * NVP * VC].bitcast(f32).rearrange("p (v c) -> p v c", c=VC)
        starts = sb("starts", [P, NVP], f32)
        bmax1 = sb("bmax1", [P, H], f32)
        bmax = sb("bmax", [P, H], f32)
        bound = sb("bound", [P, NT, H], f32)
        cnt = sb("cnt", [P, NV], f32)
        cnt0 = sb("cnt0", [P, 1], f32)
        miss = sb("miss", [P, NT], f32)
        missmax = sb("missmax", [P, NT], f32)
        missi = sb("missi", [P, NT], i32)
        edges = sb("edges", [NV, 1], f32)
        cntstep = sb("cntstep", [P, NV], f32)
        steplhs = sb("steplhs", [NV, P], f32)
        nbrep = sb("nbrep", [NV, P], f32)
        groupbase = sb("groupbase", [P, SW], f32)
        nbi = sb("nbi", [NV, 1], i32)
        nb = sb("nb", [NV, 1], f32)
        cum = sb("cum", [NV, 1], f32)
        sched = sb("sched", [1, 2, GS + NMAX], i32)
        vflat = V[:].rearrange("p v c -> p (v c)")
        startof = vflat[:, 0:NMAX]
        batchof = vflat[:, NMAX:NMAX + NMAX // 2].bitcast(bf16)
        iters = sb("iters", [1, 1], i32)
        reach = sb("reach", [P, 2, GS * P], f32)
        rank = sb("rank", [P, GS], f32)
        hit = sb("hit", [P, GS, K], f32)
        val = sb("val", [P, GS], f32)
        node1 = sb("node1", [P, GS], f32)
        idx = sb("idx", [P, RING, GS], i32)
        sel = sb("sel", [P, RING, GS, P], f32)
        G = aj[:].rearrange("p a n -> p (a n)")[:, 0:RING * GS * TR].bitcast(f32).rearrange("p (u g c) -> p u g c", u=RING, g=GS)
        z = sb("z", [P, GS, H], f32)
        z2 = sb("z2", [P, GS, H], f32)
        adj4 = aj[:, 0, :]
        sign4 = sg[:, 0, :]
        G4 = aj[:, 1, 0:8 * TR].bitcast(f32).rearrange("p (g c) -> p g c", c=TR)
        l8 = sb("l8", [P, 8], f32)
        idx8 = sb("idx8", [P, 8], i32)
        z8 = sb("z8", [P, 8, H], f32)
        most = sb("most", [P, 1], f32)
        count4 = sb("count4", [P, 1], f32)
        steps4 = sb("steps4", [1, 1], i32)
        zero = sb("zero", [P, P], bf16)
        zrow = sb("zrow", [P, HALF], bf16)
        nobody = sb("nobody", [1, TR], f32)
        acc = sb("acc", [P, 2, HALF], f32)
        xo = sb("xo", [P, D], f32)
        ob = sb("ob", [P, D], f32)
        den = sb("den", [P, H], f32)
        rden = sb("rden", [P, H], f32)
        minus1 = sb("minus1", [P, H], f32)

        psT, psH, psAD = pb("psT", [P, 512]), pb("psH", [P, 512]), pb("psAD", [P, 2, 512])
        psW = pb("psW", [P, 1024])
        psX = pb("psX", [P, 512])
        psY = pb("psY", [P, 512])
        psA, psS = psAD[:, 0, :], psAD[:, 1, :]
        fetchd = [psT, psH, psX, psY]

        def halves(rows, what):
            r = rows.rearrange("p g (a c) -> p g a c", a=2) if len(rows.shape) == 3 else rows.rearrange("p (a c) -> p a c", a=2)
            cut = slice(0, D // 2) if what == "values" else slice(D // 2, HALF)
            return r[..., cut]

        reachn, endsn = reach[0:NV, 0, 0:SW], reach[0:NV, 1, 0:SW]
        s = {}

        def S(name):
            if name not in s:
                s[name] = sem(name)
            return s[name]

        for name in ("const_in", "weights_in", "wt_done", "wt_copied", "awd_done", "wa_done", "bias_done",
                     "x_in0", "x_in1", "adj_in0", "adj_in1", "mean_ready", "relu_done", "sd_ready", "turned",
                     "ht_ready", "hm_done", "row_ready", "row_out0", "row_out1", "sign_done", "packed",
                     "words_used", "dve", "init", "lists_done", "s2", "bmax_done", "s2pe", "sched_done",
                     "diffs", "diffs_used", "reach_ready", "fetched", "idx_ready", "z_ready", "prob_ready",
                     "y_ready", "summed", "flushed", "x_again", "x_first", "out_ready", "out_done", "flag_done",
                     "passed", "drained", "acc_free", "acc_saved", "acc_ready", "x_there", "final", "nobody_out", "flags_ready", "t4_adj", "t4_x", "t4_sign", "t4_packed",
                     "t4_count", "t4_most", "t4_steps_pe", "t4_steps_act", "t4_steps_pool", "t4_idx", "t4_rows", "t4_z", "t4_prob",
                     "t4_y", "t4_summed", "t4_out", "t4_stored", "g_in0", "g_in1", "g_in2", "g_in3", "pool"):
            S(name)

        block = ctx.enter_context(nc.Block())

        class Chain:

            def __init__(self, eng, name):
                self.eng, self.sem = eng, S(name)

            def step(self, ins):
                ins.then_inc(self.sem, 1)
                self.eng.wait_ge(self.sem, 1)
                self.eng.sem_inc(self.sem, -1)

        def take(eng, name, count=1):
            eng.wait_ge(S(name), count)
            eng.sem_inc(S(name), -count)

        class Landed:

            def __init__(self, eng, name, each):
                self.eng, self.name, self.each = eng, name, each
                self.reg = eng.alloc_register(f"{name}_{each}_count")
                eng.reg_mov(self.reg, 0)

            def wait(self):
                self.eng.reg_add(self.reg, self.reg, self.each)
                self.eng.wait_ge(S(self.name), self.eng.snap(self.reg)).then_inc(S("passed"), 1)

        def own_wait(eng, name, value):
            eng.wait_ge(S(name), value).then_inc(S("passed"), 1)

        def load(eng, engine, values, top):
            _, got = nc.values_load_multi_w_load_instructions(
                values, engines=[engine], min_val=0, max_val=top,
                skip_runtime_bounds_check_because="the table holds counts of lists, which stage 2 made, up to this one")
            return got

        def padded(step):
            return bass.ds(step * GS, GS)

        @block.sync
        def _(sp):
            for k in const:
                sp.dma_start(C[k][:], const[k]).then_inc(S("const_in"), 16)
            sp.dma_start(wraw[:], W.rearrange("(c p) i -> p c i", p=P)).then_inc(S("weights_in"), 16)
            sp.dma_start(aw2[:], aw.rearrange("h d k -> (h d) k").rearrange("(c p) k -> p c k", p=P)).then_inc(S("weights_in"), 16)
            sp.dma_start(bcol[:], b.rearrange("(c p) -> p c", p=P), allow_slow_non_contiguous=True).then_inc(S("weights_in"), 16)
            sp.dma_start(bias[:], b.rearrange("(a n) -> a n", a=1).to_broadcast([P, D])).then_inc(S("weights_in"), 16)

            sp.wait_ge(S("init"), 1)
            sp.dma_start(table[TOP:TOP + 1, :], nobody[:]).then_inc(S("nobody_out"), 16)

            def store_row(t, par):
                sp.wait_ge(S("row_ready"), t + 1)
                sp.dma_start(table[bass.ds(t * P, P), :], trow[:, par, :]).then_inc(S(f"row_out{par}"), 16)

            def body(t, par, first):
                if not first:
                    sp.wait_ge(S("sign_done"), t - 1)
                sp.dma_start(aj[:, par, :], adj[bass.ds(t * P, P), :]).then_inc(S(f"adj_in{par}"), 16)
                if not first:
                    sp.wait_ge(S("relu_done"), t - 1)
                sp.dma_start(xt[:, par, :], x[bass.ds(t * P, P), :]).then_inc(S(f"x_in{par}"), 16)
                if not first:
                    store_row(t - 2, par)

            body(0, 0, True)
            body(1, 1, True)
            with sp.Fori(0, (NT - 2) // 2) as i:
                body(i * 2 + 2, 0, False)
                body(i * 2 + 3, 1, False)
            store_row(NT - 2, 0)
            store_row(NT - 1, 1)

            sp.dma_start(xo[:], x[0:P, :]).then_inc(S("x_first"), 16)
            sp.wait_ge(S("x_first"), 16)
            sp.sem_inc(S("x_there"), 1)
            with sp.Fori(0, NT - 1) as r:
                sp.wait_ge(S("out_ready"), r + 1)
                sp.dma_start(xo[:], x[bass.ds(r * P + P, P), :]).then_inc(S("x_again"), 16)
                sp.dma_start(out[bass.ds(r * P, P), :], ob[:]).then_inc(S("out_done"), 16)
                own_wait(sp, "x_again", r * 16 + 16)
                own_wait(sp, "out_done", r * 16 + 16)
                sp.sem_inc(S("x_there"), 1)
            sp.wait_ge(S("out_ready"), NT)
            sp.dma_start(out[(NT - 1) * P:NT * P, :], ob[:]).then_inc(S("out_done"), 16)
            sp.wait_ge(S("out_done"), 16 * NT)
            sp.wait_ge(S("nobody_out"), 16)

            sp.wait_ge(S("drained"), 1)
            stored = Landed(sp, "t4_stored", 16)
            with sp.Fori(0, NT) as t:
                flagged = sp.value_load(missi[0:1, bass.ds(t, 1)], min_val=0, max_val=1)
                with sp.If(flagged > 0):
                    sp.dma_start(adj4, adj[bass.ds(t * P, P), :]).then_inc(S("t4_adj"), 16)
                    sp.dma_start(xo[:], x[bass.ds(t * P, P), :]).then_inc(S("t4_x"), 16)
                    take(sp, "t4_out")
                    sp.dma_start(out[bass.ds(t * P, P), :], ob[:]).then_inc(S("t4_stored"), 16)
                    stored.wait()

        @block.scalar
        def _(act):
            for c in range(KC):
                act.wait_ge(S("wt_done"), c + 1)
                nc.scalar.activation(wt[:, c, :], [psT, psH, psX, psY][c][:], ACT.Copy).then_inc(S("wt_copied"), 1)
            act.wait_ge(S("init"), 1)

            def body(t, par, k, first=False):
                act.wait_ge(S("mean_ready"), t + 1)
                if not first:
                    act.wait_ge(S("turned"), t)
                nc.scalar.activation(hn[:], xt[:, par, :], ACT.Relu, bias=negm[:, par:par + 1]).then_inc(S("relu_done"), 1)
                nc.scalar.activation(sd[:, par:par + 1], mv[:, par, 1:2], ACT.Sqrt, bias=epsc[:]).then_inc(S("sd_ready"), 1)
                act.wait_ge(S("turned"), t + 1)
                if not first:
                    act.wait_ge(S("hm_done"), t)
                nc.scalar.activation(ht[:].rearrange("p c n -> p (c n)"), psT[:], ACT.Copy).then_inc(S("ht_ready"), 1)
                act.wait_ge(S(f"adj_in{par}"), 16 * (k + 1) if isinstance(k, int) else k * 16 + 16)
                if not (isinstance(k, int) and k == 0):
                    act.wait_ge(S("packed"), t - 1)
                nc.scalar.activation(sg[:, par, :], aj[:, par, :], ACT.Sign, bias=halfc[:],
                                     accum_out=signsum[:, bass.ds(t, 1)]).then_inc(S("sign_done"), 1)

            body(0, 0, 0, True)
            body(1, 1, 0)
            with act.Fori(0, (NT - 2) // 2) as i:
                body(i * 2 + 2, 0, i + 1)
                body(i * 2 + 3, 1, i + 1)

            act.wait_ge(S("sched_done"), 1)
            q = act.value_load(iters[0:1, 0:1], min_val=1, max_val=QMAX)

            def save(step):
                ends = load(act, mybir.EngineType.Activation, sched[0:1, 1, padded(step)], 1)
                for g in range(GS):
                    with act.If(ends[g] > 0):
                        own_wait(act, "summed", step * GS + (CLEARED - GS + g + 1))
                        take(act, "acc_free")
                        nc.scalar.activation(acc[:], psAD[:, :, 0:HALF], ACT.Copy).then_inc(S("acc_saved"), 1)
                        take(act, "acc_saved")
                        act.sem_inc(S("flushed"), 1)
                        act.sem_inc(S("acc_ready"), 1)

            with act.Fori(0, q) as i:
                for u in range(RING):
                    step = i * RING + u
                    act.wait_ge(S("z_ready"), step + 1)
                    nc.scalar.activation(halves(G[:, u], "scores"), z[:].rearrange("p g (a c) -> p g a c", a=2),
                                         ACT.Exp).then_inc(S("prob_ready"), 1)
                    save(step)
            save(q * RING)

            act.wait_ge(S("flags_ready"), 1)
            adj_in = Landed(act, "t4_adj", 16)
            with act.Fori(0, NT) as t:
                flagged = act.value_load(missi[0:1, bass.ds(t, 1)], min_val=0, max_val=1)
                with act.If(flagged > 0):
                    adj_in.wait()
                    nc.scalar.activation(sign4, adj4, ACT.Sign, bias=halfc[:]).then_inc(S("t4_sign"), 1)
                    with act.Fori(0, NCH):
                        take(act, "t4_steps_act")
                        steps = act.value_load(steps4[0:1, 0:1], min_val=1, max_val=BITS * CW // 8)
                        with act.Fori(0, steps):
                            take(act, "t4_z")
                            nc.scalar.activation(halves(G4, "scores"), z8[:].rearrange("p g (a c) -> p g a c", a=2),
                                                 ACT.Exp).then_inc(S("t4_prob"), 1)

        @block.tensor
        def _(pe):
            pe.wait_ge(S("const_in"), 16 * len(const))
            pe.wait_ge(S("weights_in"), 64)
            for c in range(KC):
                dst = [psT, psH, psX, psY][c]
                for o in range(KC):
                    last = nc.tensor.transpose(dst[:, o * P:(o + 1) * P], wraw[:, o, c * P:(c + 1) * P], eye[:])
                last.then_inc(S("wt_done"), 1)
            pe.wait_ge(S("awd_done"), 1)
            for c in range(KC):
                for o in range(KC):
                    nc.tensor.matmul(psA[:, c * 16:c * 16 + 16], wraw[:, o, c * P:(c + 1) * P], awd[:, o, :],
                                     start=(o == 0), stop=(o == KC - 1))
            for o in range(KC):
                last = nc.tensor.matmul(psA[:, 64:80], biasrep[:, o, :], awd[:, o, :], start=(o == 0), stop=(o == KC - 1))
            last.then_inc(S("wa_done"), 1)
            pe.wait_ge(S("bias_done"), 1)
            pe.wait_ge(S("wt_copied"), KC)

            def pack(signs):
                for lo, n in ((0, 512), (512, 256)):
                    for k in range(BITS):
                        nc.tensor.matmul(psW[:, lo:lo + n], packs[:, k, :],
                                         signs[:, k * NW + lo:k * NW + lo + n], start=(k == 0), stop=False)
                    last = nc.tensor.matmul(psW[:, lo:lo + n], ones2[:], wordrow[:, lo:lo + n],
                                            start=False, stop=True)
                return last

            def body(t, par, first=False):
                pe.wait_ge(S("relu_done"), t + 1)
                if not first:
                    pe.wait_ge(S("ht_ready"), t)
                for c in range(KC):
                    last = nc.tensor.transpose(psT[:, c * P:(c + 1) * P], hn[:, c * P:(c + 1) * P], eye[:])
                last.then_inc(S("turned"), 1)
                pe.wait_ge(S("ht_ready"), t + 1)
                if not first:
                    pe.wait_ge(S("row_ready"), t)
                for c in range(KC):
                    nc.tensor.matmul(psH[:], ht[:, c, :], wt[:, c, :], start=(c == 0), stop=(c == KC - 1))
                for c in range(KC):
                    last = nc.tensor.matmul(psS[:, 0:16], ht[:, c, :], wa[:, c, :], start=(c == 0), stop=(c == KC - 1))
                last.then_inc(S("hm_done"), 1)
                pe.wait_ge(S("sign_done"), t + 1)
                if not first:
                    pe.wait_ge(S("words_used"), t)
                pack(sg[:, par, :]).then_inc(S("packed"), 1)

            body(0, 0, True)
            body(1, 1)
            with pe.Fori(0, (NT - 2) // 2) as i:
                body(i * 2 + 2, 0)
                body(i * 2 + 3, 1)

            pe.wait_ge(S("s2"), 1)
            nc.tensor.matmul(psT[:, 0:NV], C["before"][:], cnt[:], start=True, stop=True)
            nc.tensor.matmul(psY[0:NV, 0:P], cntstep[:], C["before"][:], start=True, stop=True)
            nc.tensor.matmul(psH[0:NV, 0:1], cnt[:], C["ones"][:, 0:1], start=True, stop=True).then_inc(S("s2pe"), 1)
            pe.wait_ge(S("s2"), 2)
            nc.tensor.matmul(psX[0:NV, 0:1], C["upto"][0:NV, 0:NV], nb[:], start=True, stop=True)
            nc.tensor.matmul(psX[0:1, 1:2], nb[:], C["ones"][0:NV, 0:1], start=True, stop=True).then_inc(S("s2pe"), 1)
            for g in range(9):
                pe.wait_ge(S("s2"), 3)
                if g >= 2:
                    pe.wait_ge(S("diffs_used"), g - 1)
                nc.tensor.matmul([psA, psS][g % 2][:, 0:7 * VC], C["diff"][:],
                                 V[:, 7 * g:7 * g + 7, :].rearrange("p v c -> p (v c)"),
                                 start=True, stop=True).then_inc(S("diffs"), 1)
            for j in range(NMAX // SW):
                pe.wait_ge(S("s2"), 4 + j)
                nc.tensor.matmul(psT[0:1, 0:SW], C["ones"][0:NV, 0:1], reachn, start=True, stop=True)
                nc.tensor.matmul(psH[0:1, 0:SW], C["newrow"][:], endsn, start=True, stop=True)
                nc.tensor.matmul(psX[:, 0:SW], steplhs[:], reachn, start=True, stop=True)
                nc.tensor.matmul(psY[:, 0:SW], nbrep[:], reachn, start=True, stop=True).then_inc(S("s2pe"), 1)
            pe.wait_ge(S("sched_done"), 1)
            q = pe.value_load(iters[0:1, 0:1], min_val=1, max_val=QMAX)

            def fetch(step, u):
                own_wait(pe, "reach_ready", step + 1)
                v = load(pe, mybir.EngineType.PE, sched[0:1, 0, padded(step + 1)], NV)
                for g in range(GS):
                    last = nc.tensor.matmul(fetchd[u][:, g * VC:(g + 1) * VC], reach[:, u % 2, g * P:(g + 1) * P],
                                            Dv[:, bass.ds(v[g], 1), :].rearrange("p v c -> p (v c)"), start=True, stop=True)
                last.then_inc(S("fetched"), 1)

            def clear():
                for a in range(2):
                    last = nc.tensor.matmul(psAD[:, a, 0:HALF], zero[:], zrow[:], start=True, stop=False, skip_group_check=True)
                return last

            def add(weights, rows):
                for a in range(2):
                    last = nc.tensor.matmul(psAD[:, a, 0:HALF], weights, rows[:, a * HALF:(a + 1) * HALF],
                                            start=False, stop=False, skip_group_check=True)
                return last

            for m in range(LAG + 1):
                fetch(m, m)
            clear().then_inc(S("summed"), CLEARED)
            with pe.Fori(0, q) as i:
                for u in range(RING):
                    step = i * RING + u
                    fetch(step + (LAG + 1), (u + LAG + 1) % RING)
                    ends = load(pe, mybir.EngineType.PE, sched[0:1, 1, padded(step + 1)], 1)
                    for g in range(GS):
                        pe.wait_ge(S("y_ready"), step * GS + (g + 1))
                        add(sel[:, u, g, :], G[:, u, g, :]).then_inc(S("summed"), 1)
                        with pe.If(ends[g] > 0):
                            take(pe, "flushed")
                            clear()

            pe.wait_ge(S("flags_ready"), 1)
            with pe.Fori(0, NT) as t:
                flagged = pe.value_load(missi[0:1, bass.ds(t, 1)], min_val=0, max_val=1)
                with pe.If(flagged > 0):
                    take(pe, "t4_sign")
                    pack(sign4)
                    clear().then_inc(S("t4_packed"), 1)
                    with pe.Fori(0, NCH):
                        take(pe, "t4_steps_pe")
                        steps = pe.value_load(steps4[0:1, 0:1], min_val=1, max_val=BITS * CW // 8)
                        with pe.Fori(0, steps):
                            take(pe, "t4_y")
                            for g in range(8):
                                last = add(eye[:], G4[:, g, :])
                            last.then_inc(S("t4_summed"), 1)

        @block.vector
        def _(dve):
            ch = Chain(dve, "dve")
            v_ = nc.vector
            v_.memset(epsc[:], 1e-5)
            v_.memset(halfc[:], -0.5)
            v_.memset(V[:], 0.0)
            v_.memset(lst[:], 0.0)
            v_.memset(cntstep[:], 0.0)
            v_.memset(nobody[:, 0:TR], 0.0)
            v_.memset(sched[:, :, 0:GS], 0)
            v_.memset(zero[:], 0.0)
            v_.memset(zrow[:], 0.0)
            ch.step(v_.memset(awd[:], 0.0))
            v_.memset(halves(nobody[:], "scores"), FAR)
            dve.wait_ge(S("const_in"), 16 * len(const))
            dve.wait_ge(S("weights_in"), 64)
            for k in range(BITS):
                v_.tensor_scalar(packs[:, k, :], eye[:], float(WSC * 2 ** k), None, ALU.mult)
            v_.memset(ones2[:], 1.0)
            v_.tensor_copy(wordrow[:], C["wordrow"][:])
            v_.memset(cnt0[:], 0.0).then_inc(S("init"), 1)
            for o in range(KC):
                for half in range(2):
                    h = 2 * o + half
                    rows = slice(half * DH, (half + 1) * DH)
                    v_.tensor_copy(awd[rows, o, h:h + 1], aw2[rows, o, 0:1])
                    v_.tensor_copy(awd[rows, o, H + h:H + h + 1], aw2[rows, o, 1:2])
            v_.tensor_copy(biasrep[:], bcol[:].unsqueeze(2).to_broadcast([P, KC, P])).then_inc(S("awd_done"), 1)
            dve.wait_ge(S("wa_done"), 1)
            v_.tensor_copy(wa[:].rearrange("p c k -> p (c k)"), psA[:, 0:64])
            v_.tensor_copy(abias[:], psA[:, 64:80]).then_inc(S("bias_done"), 1)
            dve.wait_ge(S("bias_done"), 1)

            def mean(t, par, k):
                dve.wait_ge(S(f"x_in{par}"), 16 * (k + 1) if isinstance(k, int) else k * 16 + 16)
                ch.step(v_.bn_stats(stats[:, par, :], xt[:, par, :]))
                if not (isinstance(t, int) and t < 2):
                    own_wait(dve, "sd_ready", t - 1)
                ch.step(v_.bn_aggr(mv[:, par, :], stats[:, par, :]))
                v_.tensor_scalar(negm[:, par:par + 1], mv[:, par, 0:1], -1.0, None, ALU.mult).then_inc(S("mean_ready"), 1)

            def rows(t, par, k):
                own_wait(dve, "sd_ready", t + 1)
                ch.step(v_.reciprocal(rs[:, par:par + 1], sd[:, par:par + 1]))
                dve.wait_ge(S("hm_done"), t + 1)
                if k is not None:
                    dve.wait_ge(S(f"row_out{par}"), k * 16)
                v_.scalar_tensor_tensor(ab[:, bass.ds(t, 1), :].rearrange("p a c -> p (a c)"), psS[:, 0:16],
                                        rs[:, par:par + 1], abias[:], ALU.mult, ALU.add)
                v_.scalar_tensor_tensor(halves(trow[:, par, :], "scores"),
                                        psS[:, H:2 * H].rearrange("p (a c) -> p a c", a=2), rs[:, par:par + 1],
                                        abias[:, H:2 * H].rearrange("p (a c) -> p a c", a=2), ALU.mult, ALU.add)
                v_.scalar_tensor_tensor(halves(trow[:, par, :], "values"),
                                        psH[:].rearrange("p (a c) -> p a c", a=2), rs[:, par:par + 1],
                                        bias[:].rearrange("p (a c) -> p a c", a=2),
                                        ALU.mult, ALU.add).then_inc(S("row_ready"), 1)

            def candidates(src, nw):
                first = v_.tensor_scalar(wint[:, 0:nw], src, float(WSC * 255), None, ALU.add)
                ch.step(first)
                v_.tensor_tensor(bits[:, :, 0:nw], wint[:, 0:nw].unsqueeze(1).to_broadcast([P, BITS, nw]),
                                 C["bitmask"][:].unsqueeze(2).to_broadcast([P, BITS, nw]), ALU.bitwise_and)
                ch.step(v_.tensor_scalar(widx[:, 0:nw], wint[:, 0:nw], 2 * WSC - 1, None, ALU.bitwise_and))
                ch.step(v_.tensor_scalar(wneg[:, 0:nw], widx[:, 0:nw], -1.0, float(TOP), ALU.mult, ALU.add))
                ch.step(v_.tensor_tensor(cand[:, :, 0:nw], wneg[:, 0:nw].unsqueeze(1).to_broadcast([P, BITS, nw]),
                                         C["bitcol"][:].unsqueeze(2).to_broadcast([P, BITS, nw]), ALU.subtract))
                ch.step(v_.scalar_tensor_tensor(cand[:, :, 0:nw], bits[:, :, 0:nw], 0.0, cand[:, :, 0:nw],
                                                ALU.is_gt, ALU.mult))

            def expand(src, nw, nl, dst_v):
                candidates(src, nw)
                for r in range(nl):
                    ch.step(v_.max(lst[:, 8 * r:8 * r + 8], cand[:, :, 0:nw]))
                    if r < nl - 1:
                        ch.step(v_.match_replace(cand[:, :, 0:nw], lst[:, 8 * r:8 * r + 8], cand[:, :, 0:nw], 0.0))
                ch.step(v_.tensor_copy(V[:, bass.ds(dst_v, 1), 18:18 + 8 * nl].rearrange("p a c -> p (a c)"), lst[:, 0:8 * nl]))

            def lists(t):
                own_wait(dve, "packed", t + 1)
                for c in range(NCH):
                    last = v_.max(tops[:, 8 * c:8 * c + 8], psW[:, CW * c:CW * c + CW])
                last.then_inc(S("words_used"), 1)
                own_wait(dve, "words_used", t + 1)
                for r in range(LW // 8):
                    ch.step(v_.max(wl[:, 8 * r:8 * r + 8], tops[:]))
                    if r < LW // 8 - 1:
                        ch.step(v_.match_replace(tops[:], wl[:, 8 * r:8 * r + 8], tops[:], GONE))
                expand(wl[:], LW, LW // 8, t + (NCH - 1))

            mean(0, 0, 0)
            mean(1, 1, 0)
            rows(0, 0, None)
            dve.wait_ge(S("packed"), 1)
            with dve.Fori(0, NCH) as c:
                expand(psW[:, bass.ds(c * CW, CW)], CW, K // 8, c)
            v_.tensor_copy(cnt0[:], psW[:, 0:1]).then_inc(S("words_used"), 1)
            mean(2, 0, 1)
            rows(1, 1, None)
            lists(1)
            with dve.Fori(0, (NT - 4) // 2) as i:
                for par in range(2):
                    t = i * 2 + (2 + par)
                    mean(t + 1, 1 - par, i + 1 + par)
                    rows(t, par, i + 1)
                    lists(t)
            mean(NT - 1, 1, NT // 2 - 1)
            rows(NT - 2, 0, NT // 2 - 1)
            lists(NT - 2)
            rows(NT - 1, 1, NT // 2 - 1)
            lists(NT - 1)

            ch.step(v_.tensor_reduce(bmax1[:], ab[:, :, H:2 * H].rearrange("p t h -> p h t"), AX.X, ALU.max))
            dve.wait_ge(S("sign_done"), NT)
            dve.wait_ge(S("packed"), NT)
            v_.memset(Dv[:, NV, :], 0.0)
            ones4 = aj[:, 1, 0:NV * K].bitcast(f32).rearrange("p (v k) -> p v k", k=K)
            ch.step(v_.tensor_scalar(ones4, V[:, 0:NV, 18:VC], 0.0, None, ALU.is_gt))
            ch.step(v_.tensor_reduce(cnt[:], ones4, AX.X, ALU.add))
            v_.tensor_tensor(cntstep[:, 0:NV - 1], cnt[:, 1:NV], cnt[:, 0:NV - 1], ALU.subtract).then_inc(S("s2"), 1)
            ch.step(v_.tensor_reduce(cnt0[:], cnt[:, 0:NCH], AX.X, ALU.add))
            ch.step(v_.tensor_scalar(miss[:], signsum[:], 0.5, float(N // 2), ALU.mult, ALU.add))
            v_.tensor_tensor(miss[:, 0:1], miss[:, 0:1], cnt0[:], ALU.subtract)
            ch.step(v_.tensor_tensor(miss[:, 1:NT], miss[:, 1:NT], cnt[:, NCH:NV], ALU.subtract))
            v_.tensor_copy(cnt0[:], cnt0[:]).then_inc(S("lists_done"), 1)
            dve.wait_ge(S("s2pe"), 1)
            ch.step(v_.tensor_scalar(nbi[:], psH[0:NV, 0:1], float(P - 1), None, ALU.add))
            ch.step(v_.tensor_scalar(nbi[:], nbi[:], P.bit_length() - 1, None, ALU.arith_shift_right))
            ch.step(v_.tensor_copy(nb[:], nbi[:]))
            ch.step(v_.tensor_tensor(nb[:], nb[:], C["newrow"][:], ALU.max))
            v_.tensor_copy(nbrep[:], nb[:].to_broadcast([NV, P]))
            v_.scalar_tensor_tensor(steplhs[:], nb[:].to_broadcast([NV, P]), float(P), psY[0:NV, 0:P],
                                    ALU.mult, ALU.add).then_inc(S("s2"), 1)
            ch.step(v_.tensor_copy(starts[:, 0:NV], psT[:, 0:NV]))
            v_.tensor_scalar(groupbase[:], C["count"][:, 0:SW], float(-P), starts[:, 0:1], ALU.mult, ALU.add)
            v_.tensor_copy(V[:, 0:NV, 0:1].rearrange("p v c -> p (v c)"), starts[:, 0:NV])
            v_.tensor_copy(V[:, 0:NV, 1:2].rearrange("p v c -> p (v c)"), C["row1"][:].to_broadcast([P, NV]))
            v_.tensor_copy(V[:, 0:NCH, 2:2 + H], ab[:, 0:1, 0:H].to_broadcast([P, NCH, H]))
            v_.tensor_copy(V[:, NCH:NV, 2:2 + H], ab[:, 1:NT, 0:H])
            dve.wait_ge(S("bmax_done"), 1)
            ch.step(v_.tensor_tensor(bound[:], ab[:, :, 0:H], bmax[:].unsqueeze(1).to_broadcast([P, NT, H]), ALU.add))
            ch.step(v_.scalar_tensor_tensor(bound[:], bound[:], ALPHA, bound[:], ALU.mult, ALU.max))
            ch.step(v_.tensor_scalar(bound[:], bound[:], -HEADROOM, None, ALU.add))
            v_.tensor_copy(V[:, 0:NCH, 2 + H:2 + 2 * H], bound[:, 0:1, :].to_broadcast([P, NCH, H]))
            v_.tensor_copy(V[:, NCH:NV, 2 + H:2 + 2 * H], bound[:, 1:NT, :]).then_inc(S("s2"), 1)
            dve.wait_ge(S("s2pe"), 2)
            ch.step(v_.tensor_copy(cum[:], psX[0:NV, 0:1]))
            ch.step(v_.tensor_scalar(iters[:], psX[0:1, 1:2], float(RING * GS - 1), None, ALU.add))
            ch.step(v_.tensor_scalar(iters[:], iters[:], (RING * GS).bit_length() - 1, None, ALU.arith_shift_right))
            for g in range(9):
                dve.wait_ge(S("diffs"), g + 1)
                v_.tensor_copy(Dv[:, 7 * g:7 * g + 7, :].rearrange("p v c -> p (v c)"),
                               [psA, psS][g % 2][:, 0:7 * VC]).then_inc(S("diffs_used"), 1)
            for j in range(NMAX // SW):
                v_.tensor_scalar(reachn, C["count"][0:NV, 0:SW], float(j * SW), cum[:], ALU.add, ALU.is_ge)
                v_.tensor_scalar(endsn, C["count"][0:NV, 1:SW + 1], float(j * SW), cum[:], ALU.add,
                                 ALU.is_equal).then_inc(S("s2"), 1)
                dve.wait_ge(S("s2pe"), 3 + j)
                v_.tensor_copy(sched[0:1, 0, GS + j * SW:GS + (j + 1) * SW], psT[0:1, 0:SW])
                v_.tensor_copy(sched[0:1, 1, GS + j * SW:GS + (j + 1) * SW], psH[0:1, 0:SW])
                v_.scalar_tensor_tensor(startof[:, j * SW:(j + 1) * SW], psX[:, 0:SW], float(-P * SW * j),
                                        groupbase[:], ALU.add, ALU.add)
                last = v_.scalar_tensor_tensor(batchof[:, j * SW:(j + 1) * SW], C["count"][:, 0:SW], float(SW * j),
                                               psY[:, 0:SW], ALU.add, ALU.subtract)
            last.then_inc(S("sched_done"), 1)
            dve.wait_ge(S("sched_done"), 1)

            q = dve.value_load(iters[0:1, 0:1], min_val=1, max_val=QMAX)

            def reach_of(step, u):
                v_.tensor_tensor(reach[:, u % 2, :].rearrange("p (g e) -> p g e", g=GS),
                                 C["count"][:, 0:P].unsqueeze(1).to_broadcast([P, GS, P]),
                                 startof[:, bass.ds(step * GS, GS)].unsqueeze(2).to_broadcast([P, GS, P]),
                                 ALU.is_ge).then_inc(S("reach_ready"), 1)

            def fetched(u):
                return fetchd[u][:, 0:GS * VC].rearrange("p (g c) -> p g c", g=GS)

            def choose(step, u):
                own_wait(dve, "fetched", step + 1)
                F = fetched(u)
                ch.step(v_.scalar_tensor_tensor(rank[:], batchof[:, bass.ds(step * GS, GS)], float(P), F[:, :, 0],
                                                ALU.mult, ALU.subtract))
                ch.step(v_.tensor_tensor(hit[:], C["rankoff"][:].unsqueeze(1).to_broadcast([P, GS, K]),
                                         rank[:].unsqueeze(2).to_broadcast([P, GS, K]), ALU.is_equal))
                ch.step(v_.tensor_tensor(hit[:], hit[:], F[:, :, 18:VC], ALU.mult))
                ch.step(v_.tensor_reduce(val[:], hit[:], AX.X, ALU.add))
                if not isinstance(step, int):
                    own_wait(dve, "summed", step * GS + (CLEARED - (RING - 1) * GS))
                v_.tensor_scalar(idx[:, u, :], val[:], -1.0, float(TOP), ALU.mult, ALU.add).then_inc(S("idx_ready"), 1)
                ch.step(v_.scalar_tensor_tensor(node1[:], val[:], 0.0, F[:, :, 1], ALU.is_gt, ALU.mult))
                v_.tensor_tensor(sel[:, u, :, :], C["count"][:, 1:P + 1].unsqueeze(1).to_broadcast([P, GS, P]),
                                 node1[:].unsqueeze(2).to_broadcast([P, GS, P]), ALU.is_equal)

            def scores(u, gathers):
                dve.wait_ge(S(f"g_in{u}"), gathers)
                F = fetched(u)
                ch.step(v_.tensor_tensor(z2[:].rearrange("p g (a c) -> p g a c", a=2), halves(G[:, u], "scores"),
                                         F[:, :, 2:2 + H].rearrange("p g (a c) -> p g a c", a=2), ALU.add))
                ch.step(v_.scalar_tensor_tensor(z2[:], z2[:], ALPHA, z2[:], ALU.mult, ALU.max))
                v_.tensor_tensor(z[:], z2[:], F[:, :, 2 + H:2 + 2 * H], ALU.subtract).then_inc(S("z_ready"), 1)

            def weigh(row):
                y = halves(row, "values").rearrange("p a (h d) -> p a h d", d=DH)
                return v_.tensor_tensor(y, y, halves(row, "scores").unsqueeze(3).to_broadcast([P, 2, H // 2, DH]), ALU.mult)

            for m in range(LAG):
                reach_of(m, m)
            for m in range(LAG):
                choose(m, m)
                if m == 0:
                    reach_of(LAG, LAG)
            with dve.Fori(0, q) as i:
                for u in range(RING):
                    step = i * RING + u
                    scores(u, i * (16 * GS) + 16 * GS)
                    reach_of(step + (LAG + 1), (u + LAG + 1) % RING)
                    choose(step + LAG, (u + LAG) % RING)
                    dve.wait_ge(S("prob_ready"), step + 1)
                    for g in range(GS):
                        weigh(G[:, u, g, :]).then_inc(S("y_ready"), 1)

            dve.wait_ge(S("flags_ready"), 1)
            dve.wait_ge(S("drained"), 1)
            rows_in = Landed(dve, "t4_rows", 8 * 16)
            x_in = Landed(dve, "t4_x", 16)
            with dve.Fori(0, NT) as t:
                flagged = dve.value_load(missi[0:1, bass.ds(t, 1)], min_val=0, max_val=1)
                with dve.If(flagged > 0):
                    take(dve, "t4_packed")
                    with dve.Fori(0, NCH) as c:
                        candidates(psW[:, bass.ds(c * CW, CW)], CW)
                        ch.step(v_.tensor_scalar(bits[:], cand[:], 0.0, None, ALU.is_gt))
                        v_.tensor_reduce(count4[:], bits[:].rearrange("p k w -> p (k w)"), AX.X,
                                         ALU.add).then_inc(S("t4_count"), 1)
                        take(dve, "t4_most")
                        ch.step(v_.tensor_scalar(steps4[:], most[0:1, :], 1.0, 7.0, ALU.max, ALU.add))
                        ch.step(v_.tensor_scalar(steps4[:], steps4[:], 3, None, ALU.arith_shift_right))
                        for name in ("t4_steps_pe", "t4_steps_act", "t4_steps_pool"):
                            dve.sem_inc(S(name), 1)
                        steps = dve.value_load(steps4[0:1, 0:1], min_val=1, max_val=BITS * CW // 8)
                        with dve.Fori(0, steps):
                            ch.step(v_.max(l8[:], cand[:]))
                            v_.tensor_scalar(idx8[:], l8[:], -1.0, float(TOP), ALU.mult, ALU.add).then_inc(S("t4_idx"), 1)
                            ch.step(v_.match_replace(cand[:], l8[:], cand[:], 0.0))
                            rows_in.wait()
                            ch.step(v_.tensor_tensor(z8[:].rearrange("p g (a c) -> p g a c", a=2), halves(G4, "scores"),
                                                     ab[:, bass.ds(t, 1), 0:H].rearrange("p g (a c) -> p g a c", a=2).to_broadcast([P, 8, 2, H // 2]), ALU.add))
                            ch.step(v_.scalar_tensor_tensor(z8[:], z8[:], ALPHA, z8[:], ALU.mult, ALU.max))
                            v_.tensor_tensor(z8[:], z8[:], bound[:, bass.ds(t, 1), :].to_broadcast([P, 8, H]),
                                             ALU.subtract).then_inc(S("t4_z"), 1)
                            take(dve, "t4_prob")
                            for g in range(8):
                                last = weigh(G4[:, g, :])
                            last.then_inc(S("t4_y"), 1)
                            take(dve, "t4_summed")
                    ch.step(v_.tensor_scalar(den[:].rearrange("p (a c) -> p a c", a=2), psAD[:, :, D // 2:HALF], 1e-37, None, ALU.max))
                    ch.step(v_.reciprocal(rden[:], den[:]))
                    x_in.wait()
                    ch.step(v_.tensor_tensor(ob[:].rearrange("p (a h d) -> p a h d", a=2, d=DH),
                                             psAD[:, :, 0:D // 2].rearrange("p a (h d) -> p a h d", d=DH),
                                             rden[:].rearrange("p (a h) -> p a h", a=2).unsqueeze(3).to_broadcast([P, 2, H // 2, DH]), ALU.mult))
                    v_.tensor_tensor(ob[:], ob[:], xo[:], ALU.add).then_inc(S("t4_out"), 1)

        @block.gpsimd
        def _(pool):
            pool.wait_ge(S("lists_done"), 1)
            nc.gpsimd.partition_all_reduce(bmax[:], bmax1[:], P, bass.bass_isa.ReduceOp.max).then_inc(S("bmax_done"), 1)
            nc.gpsimd.partition_all_reduce(missmax[:], miss[:], P, bass.bass_isa.ReduceOp.max).then_inc(S("pool"), 1)
            pool.wait_ge(S("pool"), 1)
            nc.gpsimd.tensor_scalar(missi[:], missmax[:], 0.0, None, ALU.is_gt).then_inc(S("flags_ready"), 1)
            pool.wait_ge(S("flags_ready"), 1)
            for par in range(2):
                pool.wait_ge(S(f"row_out{par}"), 16 * NT // 2)
            pool.wait_ge(S("sched_done"), 1)
            q = pool.value_load(iters[0:1, 0:1], min_val=1, max_val=QMAX)

            def gather(step, u):
                own_wait(pool, "idx_ready", step + 1)
                for g in range(GS):
                    nc.gpsimd.indirect_dma_start(
                        out=G[:, u, g, :], out_offset=None, in_=table,
                        in_offset=bass.IndirectOffsetOnAxis(ap=idx[:, u, g:g + 1], axis=0),
                        bounds_check=TOP, oob_is_err=False).then_inc(S(f"g_in{u}"), 16)

            link = Chain(pool, "final").step
            link(nc.gpsimd.memset(minus1[:], -1.0))

            def finish(step):
                ends = load(pool, mybir.EngineType.Pool, sched[0:1, 1, padded(step)], 1)
                for g in range(GS):
                    with pool.If(ends[g] > 0):
                        take(pool, "acc_ready")
                        link(nc.gpsimd.tensor_scalar(den[:].rearrange("p (a c) -> p a c", a=2), acc[:, :, D // 2:HALF],
                                                     1e-37, None, ALU.max))
                        link(nc.gpsimd.tensor_tensor(rden[:], den[:], minus1[:], ALU.pow))
                        link(nc.gpsimd.tensor_tensor(den[:], den[:], rden[:], ALU.mult))
                        link(nc.gpsimd.tensor_scalar(den[:], den[:], -1.0, 2.0, ALU.mult, ALU.add))
                        link(nc.gpsimd.tensor_tensor(rden[:], rden[:], den[:], ALU.mult))
                        take(pool, "x_there")
                        link(nc.gpsimd.tensor_tensor(ob[:].rearrange("p (a h d) -> p a h d", a=2, d=DH),
                                                     acc[:, :, 0:D // 2].rearrange("p a (h d) -> p a h d", d=DH),
                                                     rden[:].rearrange("p (a h) -> p a h", a=2).unsqueeze(3).to_broadcast([P, 2, H // 2, DH]),
                                                     ALU.mult))
                        pool.sem_inc(S("acc_free"), 1)
                        nc.gpsimd.tensor_tensor(ob[:], ob[:], xo[:], ALU.add).then_inc(S("out_ready"), 1)

            pool.wait_ge(S("nobody_out"), 16)
            pool.sem_inc(S("acc_free"), 1)
            for m in range(LAG):
                gather(m, m)
            with pool.Fori(0, q) as i:
                for u in range(RING):
                    gather(i * RING + (u + LAG), (u + LAG) % RING)
                    finish(i * RING + u)
            finish(q * RING)
            for m in range(LAG):
                own_wait(pool, f"g_in{m}", q * (16 * GS) + 16 * GS)
            own_wait(pool, "summed", q * (RING * GS) + CLEARED)
            pool.sem_inc(S("drained"), 1)

            with pool.Fori(0, NT) as t:
                flagged = pool.value_load(missi[0:1, bass.ds(t, 1)], min_val=0, max_val=1)
                with pool.If(flagged > 0):
                    with pool.Fori(0, NCH):
                        take(pool, "t4_count")
                        nc.gpsimd.partition_all_reduce(most[:], count4[:], P, bass.bass_isa.ReduceOp.max).then_inc(S("t4_most"), 1)
                        take(pool, "t4_steps_pool")
                        steps = pool.value_load(steps4[0:1, 0:1], min_val=1, max_val=BITS * CW // 8)
                        with pool.Fori(0, steps):
                            take(pool, "t4_idx")
                            for g in range(8):
                                nc.gpsimd.indirect_dma_start(
                                    out=G4[:, g, :], out_offset=None, in_=table,
                                    in_offset=bass.IndirectOffsetOnAxis(ap=idx8[:, g:g + 1], axis=0),
                                    bounds_check=TOP, oob_is_err=False).then_inc(S("t4_rows"), 16)


_INS = ["x", "adj", "L0_gnn_W", "L0_gnn_b", "L0_gnn_aw"]
_OUTS = [((N, D), "float32")]


def kernel(**inputs):
    import numpy as _np
    import concourse.bacc as _bacc
    from concourse import mybir as _mybir
    from concourse.bass_utils import run_bass_kernel_spmd as _run

    nc = _bacc.Bacc("TRN2", target_bir_lowering=False, num_devices=1)
    arrays, args, const = {}, [], {}
    for name in _INS:
        a = _np.ascontiguousarray(inputs[name])
        arrays[f"in_{name}_dram"] = a
        args.append(nc.dram_tensor(f"in_{name}_dram", a.shape, _mybir.dt.from_np(a.dtype), kind="ExternalInput").ap())
    for name, a in constants().items():
        arrays[f"const_{name}_dram"] = a
        const[name] = nc.dram_tensor(f"const_{name}_dram", a.shape, _mybir.dt.from_np(a.dtype), kind="ExternalInput").ap()
    outs = []
    for i, (shape, dtype) in enumerate(_OUTS):
        dt = _mybir.dt.from_np(_np.dtype(dtype))
        outs.append(nc.dram_tensor(f"out_{i}_dram", shape, dt, kind="ExternalOutput").ap())
    build(nc, *args, const, *outs)
    r = _run(nc, [arrays], core_ids=[0])
    got = tuple(r.results[0][f"out_{i}_dram"] for i in range(len(_OUTS)))
    return got[0]
```

```python
import concourse.bass as bass
from concourse import mybir
from contextlib import ExitStack


N, D, H, DH = 6144, 512, 8, 64
P = 128
NT = N // P
KC = D // P
BITS = 8
NW = N // BITS
NCH = 16
CW = NW // NCH
FIRST, SECOND, MIDDLE, LATE = 5, 5, 4, 3
MIDDLE_FROM, LATE_FROM = 4, 12
K = 8 * FIRST
TOP = N
WSC = 1024
NV = NCH + NT - 1
NVP = NV + 1
VC = 2 + 2 * H + K
HALF = D // 2 + H // 2
TR = 2 * HALF
GS = 4
SW = 480
NMAX = 4 * SW
LEAD = 3
RING = 4
EARLY = 1
CLEARED = GS
GMAX = 8 * (NCH * FIRST + (MIDDLE_FROM - 1) * SECOND + (LATE_FROM - MIDDLE_FROM) * MIDDLE + (NT - LATE_FROM) * LATE)
QMAX = -(-GMAX // (GS * RING))
assert (QMAX * RING + LEAD + 2) * GS <= NMAX
ALPHA = 0.2
HEADROOM = 40.0
GONE = -3.0e5
FAR = -1.0e30


def constants():
    import numpy as np

    f = np.float32
    eye = np.eye(P, dtype=f)
    c = {}
    c["eye"] = eye
    w = np.arange(NW)
    c["wordrow"] = np.stack([w // 256 * 256, w % 256]).astype(f)
    c["bitmask"] = np.tile((1 << (11 + np.arange(BITS))).astype(np.int32), (P, 1))
    c["bitcol"] = np.tile((NW * np.arange(BITS)).astype(f), (P, 1))
    c["count"] = np.tile(np.arange(SW + 1).astype(f), (P, 1))
    c["before"] = (np.arange(P)[:, None] < np.arange(P)[None, :]).astype(f)
    c["diff"] = eye - np.eye(P, k=1, dtype=f)
    c["upto"] = (np.arange(P)[:, None] <= np.arange(P)[None, :]).astype(f)
    c["row1"] = np.arange(1, P + 1, dtype=f)[:, None].copy()
    c["rankoff"] = (np.arange(K)[None, :] - np.arange(P)[:, None]).astype(f)
    v = np.arange(NV)
    c["newrow"] = (v >= NCH - 1).astype(f)[:, None].copy()
    c["ones"] = np.ones((P, P), f)
    return c


def build(nc, x, adj, W, b, aw, const, out):
    f32, bf16, i32 = mybir.dt.float32, mybir.dt.bfloat16, mybir.dt.int32
    ALU, ACT, AX = mybir.AluOpType, mybir.ActivationFunctionType, mybir.AxisListType
    table = nc.dram_tensor("table", [TOP + 1, TR], f32).ap()

    ctx = ExitStack()
    with ctx:
        def sb(name, shape, dt):
            return ctx.enter_context(nc.sbuf_tensor(name, shape, dt))

        def pb(name, shape):
            return ctx.enter_context(nc.psum_tensor(name, shape, f32))

        def sem(name):
            return ctx.enter_context(nc.semaphore(name))

        C = {k: sb("c_" + k, list(const[k].shape), const[k].dtype) for k in const}
        eye = C["eye"]
        packs = sb("packs", [P, BITS, P], bf16)
        wordrow = sb("wordrow", [2, NW], bf16)
        ones2 = sb("ones2", [2, P], bf16)

        xt = sb("xt", [P, 2, D], f32)
        hn = sb("hn", [P, 2, D], f32)
        ht = sb("ht", [P, KC, P], f32)
        wraw = sb("wraw", [P, KC, D], f32)
        wt = sb("wt", [P, KC, D], f32)
        aw2 = sb("aw2", [P, KC, 2], f32)
        awd = sb("awd", [P, KC, 2 * H], f32)
        wa = sb("wa", [P, KC, 2 * H], f32)
        bcol = sb("bcol", [P, KC], f32)
        bias = sb("bias", [P, D], f32)
        biasrep = sb("biasrep", [P, KC, P], f32)
        abias = sb("abias", [P, 2 * H], f32)
        stats = sb("stats", [P, 2, 6], f32)
        mv = sb("mv", [P, 2, 2], f32)
        negm = sb("negm", [P, 2], f32)
        sd = sb("sd", [P, 2], f32)
        rs = sb("rs", [P, 2], f32)
        epsc = sb("epsc", [P, 1], f32)
        halfc = sb("halfc", [P, 1], f32)
        onec = sb("onec", [P, 1], f32)
        trow = sb("trow", [P, 2, TR], f32)
        ab = sb("ab", [P, NT, 2 * H], f32)
        aj = sb("aj", [P, 2, N], i32)
        sg = sb("sg", [P, 2, N], bf16)
        signsum = sb("signsum", [P, NT], f32)
        words0 = sb("words0", [P, NW], f32)
        tops = sb("tops", [P, 2, NCH * 8], f32)
        wl = sb("wl", [P, 2, K], f32)
        wint = sb("wint", [P, 3, CW], i32)
        widx = sb("widx", [P, 3, CW], i32)
        wneg = sb("wneg", [P, 3, CW], f32)
        bits = sb("bits", [P, 3, BITS, CW], i32)
        cand = sb("cand", [P, 3, BITS, CW], f32)
        lst = sb("lst", [P, 3, K], f32)
        V = sb("V", [P, NVP, VC], f32)
        Dv = sg[:, 0:2, :].rearrange("p a n -> p (a n)")[:, 0:2 * NVP * VC].bitcast(f32).rearrange("p (v c) -> p v c", c=VC)
        starts = sb("starts", [P, NVP], f32)
        bmax1 = sb("bmax1", [P, H], f32)
        bmax = sb("bmax", [P, H], f32)
        bound = sb("bound", [P, NT, H], f32)
        cnt = sb("cnt", [P, NV], f32)
        cnt0 = sb("cnt0", [P, 1], f32)
        miss = sb("miss", [P, NT + 1], f32)
        missmax = sb("missmax", [P, NT + 1], f32)
        missi = sb("missi", [P, NT + 1], i32)
        edges = sb("edges", [NV, 1], f32)
        cntstep = sb("cntstep", [P, NV], f32)
        steplhs = sb("steplhs", [NV, P], f32)
        stephigh = sb("stephigh", [NV, P], bf16)
        steplow = sb("steplow", [NV, P], bf16)
        nbrep = sb("nbrep", [NV, P], bf16)
        newrow16 = sb("newrow16", [NV, 1], bf16)
        ones16 = sb("ones16", [NV, 1], bf16)
        groupbase = sb("groupbase", [P, SW], f32)
        nbi = sb("nbi", [NV, 1], i32)
        nb = sb("nb", [NV, 1], f32)
        cum = sb("cum", [NV, 1], f32)
        sched = sb("sched", [1, 2, 2 * GS + NMAX], i32)
        vflat = V[:].rearrange("p v c -> p (v c)")
        startof = vflat[:, 0:NMAX]
        batchof = vflat[:, NMAX:NMAX + NMAX // 2].bitcast(bf16)
        iters = sb("iters", [1, 1], i32)
        reach = sb("reach", [P, 2, GS * P], f32)
        rank = sb("rank", [P, GS], f32)
        hit = sb("hit", [P, GS, K], f32)
        val = sb("val", [P, GS], f32)
        node1 = sb("node1", [P, GS], f32)
        idx = sb("idx", [P, RING, GS], i32)
        sel = sb("sel", [P, RING, GS, P], f32)
        G = aj[:].rearrange("p a n -> p (a n)")[:, 0:RING * GS * TR].bitcast(f32).rearrange("p (u g c) -> p u g c", u=RING, g=GS)
        acc = [aj[:].rearrange("p a n -> p (a n)")[:, RING * GS * TR:(RING + 1) * GS * TR].bitcast(f32).rearrange("p (g c) -> p g c", g=GS),
               sg[:].rearrange("p a n -> p (a n)")[:, 2 * NVP * VC:2 * NVP * VC + 2 * GS * TR].bitcast(f32).rearrange("p (g c) -> p g c", g=GS)]
        z = sb("z", [P, GS, H], f32)
        z2 = sb("z2", [P, GS, H], f32)
        adj4 = aj[:, 0, :]
        sign4 = sg[:, 0, :]
        G4 = aj[:, 1, 0:8 * TR].bitcast(f32).rearrange("p (g c) -> p g c", c=TR)
        l8 = sb("l8", [P, 8], f32)
        idx8 = sb("idx8", [P, 8], i32)
        z8 = sb("z8", [P, 8, H], f32)
        most = sb("most", [P, 1], f32)
        count4 = sb("count4", [P, 1], f32)
        steps4 = sb("steps4", [1, 1], i32)
        zero = sb("zero", [P, P], bf16)
        zrow = sb("zrow", [P, HALF], bf16)
        nobody = sb("nobody", [1, TR], f32)
        denmax = sb("denmax", [P, GS, H], f32)
        rdens = sb("rdens", [P, 2, GS, H], f32)
        xo = sb("xo", [P, D], f32)
        ob = sb("ob", [P, D], f32)
        den = sb("den", [P, H], f32)
        rden = sb("rden", [P, H], f32)

        psT, psH, psAD = pb("psT", [P, 512]), pb("psH", [P, 512]), pb("psAD", [P, 2, 512])
        psW, psV = pb("psW", [P, 1024]), pb("psV", [P, 1024])
        psX, psY = psV[:, 0:512], psV[:, 512:1024]
        psA, psS = psAD[:, 0, :], psAD[:, 1, :]
        fetchd = [psT, psH, psX, psY]

        def halves(rows, what):
            r = rows.rearrange("p g (a c) -> p g a c", a=2) if len(rows.shape) == 3 else rows.rearrange("p (a c) -> p a c", a=2)
            cut = slice(0, D // 2) if what == "values" else slice(D // 2, HALF)
            return r[..., cut]

        reachn, endsn = (reach[0:NV, a, 0:SW // 2].bitcast(bf16) for a in range(2))
        s = {}

        def S(name):
            if name not in s:
                s[name] = sem(name)
            return s[name]

        for name in ("const_in", "weights_in", "wt_done", "wt_copied", "awd_done", "wa_done", "bias_done",
                     "x_in0", "x_in1", "adj_in0", "adj_in1", "mean_ready", "relu_done", "sd_ready", "turned",
                     "ht_ready", "hm_done", "row_ready", "row_out0", "row_out1", "sign_done", "packed",
                     "words_used", "dve", "init", "lists_done", "s2", "bmax_done", "s2pe", "sched_done",
                     "diffs", "diffs_used", "reach_ready", "fetched", "idx_ready", "z_ready", "prob_ready",
                     "y_ready", "summed", "flushed", "x_again", "x_first", "out_ready", "out_done", "passed",
                     "drained", "acc_saved", "saved", "rden_ready", "finished", "x_there", "final", "act",
                     "nobody_out", "flags_ready", "t4_adj", "t4_x", "t4_sign", "t4_packed", "t4_count",
                     "t4_most", "t4_steps_pe", "t4_steps_act", "t4_steps_pool", "t4_idx", "t4_rows", "t4_z",
                     "t4_prob", "t4_y", "t4_summed", "t4_out", "t4_stored", "g_in0", "g_in1", "g_in2",
                     "g_in3", "pool", "dve_job0", "dve_job1", "dve_job2"):
            S(name)

        block = ctx.enter_context(nc.Block())

        class Chain:

            def __init__(self, eng, name):
                self.eng, self.sem = eng, S(name)

            def go(self, ins):
                ins.then_inc(self.sem, 1)

            def wait(self):
                self.eng.wait_ge(self.sem, 1)
                self.eng.sem_inc(self.sem, -1)

            def step(self, ins):
                ins.then_inc(self.sem, 1)
                self.eng.wait_ge(self.sem, 1)
                self.eng.sem_inc(self.sem, -1)

        def take(eng, name, count=1):
            eng.wait_ge(S(name), count)
            eng.sem_inc(S(name), -count)

        class Landed:

            def __init__(self, eng, name, each):
                self.eng, self.name, self.each = eng, name, each
                self.reg = eng.alloc_register(f"{name}_{each}_count")
                eng.reg_mov(self.reg, 0)

            def wait(self):
                self.eng.reg_add(self.reg, self.reg, self.each)
                self.eng.wait_ge(S(self.name), self.eng.snap(self.reg)).then_inc(S("passed"), 1)

        def own_wait(eng, name, value):
            eng.wait_ge(S(name), value).then_inc(S("passed"), 1)

        def load(eng, engine, values, top):
            _, got = nc.values_load_multi_w_load_instructions(
                values, engines=[engine], min_val=0, max_val=top,
                skip_runtime_bounds_check_because="the table holds counts of lists, which stage 2 made, up to this one")
            return got

        def groups(step, back=0):
            return bass.ds((step + (2 - back)) * GS, GS)

        @block.sync
        def _(sp):
            for k in const:
                sp.dma_start(C[k][:], const[k]).then_inc(S("const_in"), 16)
            sp.dma_start(wraw[:], W.rearrange("(c p) i -> p c i", p=P)).then_inc(S("weights_in"), 16)
            sp.dma_start(aw2[:], aw.rearrange("h d k -> (h d) k").rearrange("(c p) k -> p c k", p=P)).then_inc(S("weights_in"), 16)
            sp.dma_start(bcol[:], b.rearrange("(c p) -> p c", p=P), allow_slow_non_contiguous=True).then_inc(S("weights_in"), 16)
            sp.dma_start(bias[:], b.rearrange("(a n) -> a n", a=1).to_broadcast([P, D])).then_inc(S("weights_in"), 16)

            sp.wait_ge(S("init"), 1)
            sp.dma_start(table[TOP:TOP + 1, :], nobody[:]).then_inc(S("nobody_out"), 16)

            def body(t, first=False):
                for par in range(2):
                    if not first:
                        sp.wait_ge(S("relu_done"), t + (par - 1))
                    sp.dma_start(xt[:, par, :], x[bass.ds((t + par) * P, P), :]).then_inc(S(f"x_in{par}"), 16)
                for par in range(2):
                    if not first:
                        sp.wait_ge(S("sign_done"), t + (par - 1))
                    sp.dma_start(aj[:, par, :], adj[bass.ds((t + par) * P, P), :]).then_inc(S(f"adj_in{par}"), 16)

            body(0, True)
            with sp.Fori(0, (NT - 2) // 2) as i:
                body(i * 2 + 2)

            sp.dma_start(xo[:], x[0:P, :]).then_inc(S("x_first"), 16)
            sp.wait_ge(S("x_first"), 16)
            sp.sem_inc(S("x_there"), 1)
            with sp.Fori(0, NT - 1) as r:
                sp.wait_ge(S("out_ready"), r + 1)
                sp.dma_start(xo[:], x[bass.ds(r * P + P, P), :]).then_inc(S("x_again"), 16)
                sp.dma_start(out[bass.ds(r * P, P), :], ob[:]).then_inc(S("out_done"), 16)
                own_wait(sp, "x_again", r * 16 + 16)
                own_wait(sp, "out_done", r * 16 + 16)
                sp.sem_inc(S("x_there"), 1)
            sp.wait_ge(S("out_ready"), NT)
            sp.dma_start(out[(NT - 1) * P:NT * P, :], ob[:]).then_inc(S("out_done"), 16)
            sp.wait_ge(S("out_done"), 16 * NT)
            sp.wait_ge(S("nobody_out"), 16)

            sp.wait_ge(S("drained"), 1)
            stored = Landed(sp, "t4_stored", 16)
            some = sp.value_load(missi[0:1, NT:NT + 1], min_val=0, max_val=1)
            with sp.If(some > 0):
                with sp.Fori(0, NT) as t:
                    flagged = sp.value_load(missi[0:1, bass.ds(t, 1)], min_val=0, max_val=1)
                    with sp.If(flagged > 0):
                        sp.dma_start(adj4, adj[bass.ds(t * P, P), :]).then_inc(S("t4_adj"), 16)
                        sp.dma_start(xo[:], x[bass.ds(t * P, P), :]).then_inc(S("t4_x"), 16)
                        take(sp, "t4_out")
                        sp.dma_start(out[bass.ds(t * P, P), :], ob[:]).then_inc(S("t4_stored"), 16)
                        stored.wait()

        @block.scalar
        def _(act):
            for c in range(KC):
                act.wait_ge(S("wt_done"), c + 1)
                nc.scalar.activation(wt[:, c, :], [psT, psH, psX, psY][c][:], ACT.Copy).then_inc(S("wt_copied"), 1)
            act.wait_ge(S("init"), 1)

            def body(t, k, first=False):
                if not first:
                    act.wait_ge(S("turned"), t)
                for par in range(2):
                    act.wait_ge(S("mean_ready"), t + (par + 1))
                    nc.scalar.activation(hn[:, par, :], xt[:, par, :], ACT.Relu, bias=negm[:, par:par + 1]).then_inc(S("relu_done"), 1)
                nc.scalar.activation(sd[:], mv[:, :, 1], ACT.Sqrt, bias=epsc[:]).then_inc(S("sd_ready"), 2)
                for par in range(2):
                    act.wait_ge(S("turned"), t + (par + 1))
                    if not (first and par == 0):
                        act.wait_ge(S("hm_done"), t + par)
                    nc.scalar.activation(ht[:].rearrange("p c n -> p (c n)"), psT[:], ACT.Copy).then_inc(S("ht_ready"), 1)
                    act.wait_ge(S(f"adj_in{par}"), k)
                    if not first:
                        act.wait_ge(S("packed"), t + (par - 1))
                    nc.scalar.activation(sg[:, par, :], aj[:, par, :], ACT.Sign, bias=halfc[:],
                                         accum_out=signsum[:, bass.ds(t + par, 1)]).then_inc(S("sign_done"), 1)

            body(0, 16, True)
            with act.Fori(0, (NT - 2) // 2) as i:
                body(i * 2 + 2, i * 16 + 32)

            act.wait_ge(S("sched_done"), 1)
            q = act.value_load(iters[0:1, 0:1], min_val=1, max_val=QMAX)

            ca = Chain(act, "act")

            def reach_of(step, u):
                for g in range(GS):
                    last = nc.scalar.activation(reach[:, u % 2, g * P:(g + 1) * P], C["count"][:, 0:P], ACT.Relu,
                                                bias=startof[:, bass.ds(step * GS + g, 1)], scale=-1.0)
                ca.step(last)
                nc.scalar.activation(reach[:, u % 2, :], reach[:, u % 2, :], ACT.Relu, bias=onec[:],
                                     scale=-1.0).then_inc(S("reach_ready"), 1)

            reach_of(0, 0)
            reach_of(1, 1)
            for m in range(LEAD):
                act.wait_ge(S("fetched"), m + 1)
                reach_of(m + 2, m)

            def last_groups(step):
                return load(act, mybir.EngineType.Activation, sched[0:1, 1, groups(step, 1)], 1)

            def save(step, par, ends, some):
                for g in some:
                    with act.If(ends[g] > 0):
                        own_wait(act, "summed", step * GS + (CLEARED - GS + g + 1))
                        own_wait(act, "finished", step + 1)
                        own_wait(act, "rden_ready", step + 1)
                        nc.scalar.activation(acc[par][:, g, :].rearrange("p (a c) -> p a c", a=2), psAD[:, :, 0:HALF],
                                             ACT.Copy).then_inc(S("acc_saved"), 1)
                        take(act, "acc_saved")
                        act.sem_inc(S("flushed"), 1)
                if GS - 1 in some:
                    act.sem_inc(S("saved"), 1)

            with act.Fori(0, q) as i:
                for u in range(RING):
                    step = i * RING + u
                    ends = last_groups(step)
                    save(step, u % 2, ends, range(EARLY))
                    act.wait_ge(S("z_ready"), step + 1)
                    nc.scalar.activation(halves(G[:, u], "scores"), z[:].rearrange("p g (a c) -> p g a c", a=2),
                                         ACT.Exp).then_inc(S("prob_ready"), 1)
                    save(step, u % 2, ends, range(EARLY, GS))
                    own_wait(act, "fetched", step + (LEAD + 1))
                    reach_of(step + (LEAD + 2), u + LEAD + 2)
            save(q * RING, 0, last_groups(q * RING), range(GS))

            act.wait_ge(S("flags_ready"), 1)
            adj_in = Landed(act, "t4_adj", 16)
            some = act.value_load(missi[0:1, NT:NT + 1], min_val=0, max_val=1)
            with act.If(some > 0):
                with act.Fori(0, NT) as t:
                    flagged = act.value_load(missi[0:1, bass.ds(t, 1)], min_val=0, max_val=1)
                    with act.If(flagged > 0):
                        adj_in.wait()
                        nc.scalar.activation(sign4, adj4, ACT.Sign, bias=halfc[:]).then_inc(S("t4_sign"), 1)
                        with act.Fori(0, NCH):
                            take(act, "t4_steps_act")
                            steps = act.value_load(steps4[0:1, 0:1], min_val=1, max_val=BITS * CW // 8)
                            with act.Fori(0, steps):
                                take(act, "t4_z")
                                nc.scalar.activation(halves(G4, "scores"), z8[:].rearrange("p g (a c) -> p g a c", a=2),
                                                     ACT.Exp).then_inc(S("t4_prob"), 1)

        @block.tensor
        def _(pe):
            pe.wait_ge(S("const_in"), 16 * len(const))
            pe.wait_ge(S("weights_in"), 64)
            for c in range(KC):
                dst = [psT, psH, psX, psY][c]
                for o in range(KC):
                    last = nc.tensor.transpose(dst[:, o * P:(o + 1) * P], wraw[:, o, c * P:(c + 1) * P], eye[:])
                last.then_inc(S("wt_done"), 1)
            pe.wait_ge(S("awd_done"), 1)
            for c in range(KC):
                for o in range(KC):
                    nc.tensor.matmul(psA[:, c * 16:c * 16 + 16], wraw[:, o, c * P:(c + 1) * P], awd[:, o, :],
                                     start=(o == 0), stop=(o == KC - 1))
            for o in range(KC):
                last = nc.tensor.matmul(psA[:, 64:80], biasrep[:, o, :], awd[:, o, :], start=(o == 0), stop=(o == KC - 1))
            last.then_inc(S("wa_done"), 1)
            pe.wait_ge(S("bias_done"), 1)
            pe.wait_ge(S("wt_copied"), KC)

            def pack(signs, words):
                for lo, n in ((0, 512), (512, 256)):
                    for k in range(BITS):
                        nc.tensor.matmul(words[:, lo:lo + n], packs[:, k, :],
                                         signs[:, k * NW + lo:k * NW + lo + n], start=(k == 0), stop=False)
                    last = nc.tensor.matmul(words[:, lo:lo + n], ones2[:], wordrow[:, lo:lo + n],
                                            start=False, stop=True)
                return last

            def turn(t, par, first):
                pe.wait_ge(S("relu_done"), t + (par + 1))
                if not (first and par == 0):
                    pe.wait_ge(S("ht_ready"), t + par)
                for c in range(KC):
                    last = nc.tensor.transpose(psT[:, c * P:(c + 1) * P], hn[:, par, c * P:(c + 1) * P], eye[:])
                last.then_inc(S("turned"), 1)

            def product(t, par, first):
                pe.wait_ge(S("ht_ready"), t + (par + 1))
                if not first:
                    pe.wait_ge(S("row_ready"), t)
                for c in range(KC):
                    nc.tensor.matmul([psH[:], psA][par], ht[:, c, :], wt[:, c, :], start=(c == 0), stop=(c == KC - 1))
                for c in range(KC):
                    last = nc.tensor.matmul(psS[:, 16 * par:16 * par + 16], ht[:, c, :], wa[:, c, :],
                                            start=(c == 0), stop=(c == KC - 1), skip_group_check=True)
                last.then_inc(S("hm_done"), 1)

            def words(t, par, first):
                pe.wait_ge(S("sign_done"), t + (par + 1))
                if not first:
                    pe.wait_ge(S("words_used"), t + (par - 1))
                pack(sg[:, par, :], [psW, psV][par]).then_inc(S("packed"), 1)

            def body(t, first=False):
                turn(t, 0, first)
                product(t, 0, first)
                turn(t, 1, first)
                words(t, 0, first)
                product(t, 1, first)
                words(t, 1, first)

            body(0, True)
            with pe.Fori(0, (NT - 2) // 2) as i:
                body(i * 2 + 2)

            pe.wait_ge(S("s2"), 1)
            nc.tensor.matmul(psT[:, 0:NV], C["before"][:], cnt[:], start=True, stop=True)
            nc.tensor.matmul(psY[0:NV, 0:P], cntstep[:], C["before"][:], start=True, stop=True)
            nc.tensor.matmul(psH[0:NV, 0:1], cnt[:], C["ones"][:, 0:1], start=True, stop=True).then_inc(S("s2pe"), 1)
            pe.wait_ge(S("s2"), 2)
            nc.tensor.matmul(psX[0:NV, 0:1], C["upto"][0:NV, 0:NV], nb[:], start=True, stop=True)
            nc.tensor.matmul(psX[0:1, 1:2], nb[:], C["ones"][0:NV, 0:1], start=True, stop=True).then_inc(S("s2pe"), 1)
            pe.wait_ge(S("s2"), 3)
            for g in range(8):
                if g >= 2:
                    pe.wait_ge(S("diffs_used"), g - 1)
                nc.tensor.matmul([psA, psS][g % 2][:, 0:8 * VC], C["diff"][:],
                                 V[:, 8 * g:8 * g + 8, :].rearrange("p v c -> p (v c)"),
                                 start=True, stop=True).then_inc(S("diffs"), 1)
            for j in range(NMAX // SW):
                pe.wait_ge(S("s2"), 4 + j)
                nc.tensor.matmul(psT[0:1, 0:SW], ones16[:], reachn, start=True, stop=True)
                nc.tensor.matmul(psH[0:1, 0:SW], newrow16[:], endsn, start=True, stop=True)
                nc.tensor.matmul(psX[:, 0:SW], stephigh[:], reachn, start=True, stop=False)
                nc.tensor.matmul(psX[:, 0:SW], steplow[:], reachn, start=False, stop=True)
                nc.tensor.matmul(psY[:, 0:SW], nbrep[:], reachn, start=True, stop=True).then_inc(S("s2pe"), 1)
            pe.wait_ge(S("sched_done"), 1)
            q = pe.value_load(iters[0:1, 0:1], min_val=1, max_val=QMAX)

            def fetch(step, u):
                own_wait(pe, "reach_ready", step + 1)
                v = load(pe, mybir.EngineType.PE, sched[0:1, 0, groups(step)], NV)
                for g in range(GS):
                    last = nc.tensor.matmul(fetchd[u][:, g * VC:(g + 1) * VC], reach[:, u % 2, g * P:(g + 1) * P],
                                            Dv[:, bass.ds(v[g], 1), :].rearrange("p v c -> p (v c)"), start=True, stop=True)
                last.then_inc(S("fetched"), 1)

            def clear():
                for a in range(2):
                    last = nc.tensor.matmul(psAD[:, a, 0:HALF], zero[:], zrow[:], start=True, stop=False, skip_group_check=True)
                return last

            def add(weights, rows):
                for a in range(2):
                    last = nc.tensor.matmul(psAD[:, a, 0:HALF], weights, rows[:, a * HALF:(a + 1) * HALF],
                                            start=False, stop=False, skip_group_check=True)
                return last

            for m in range(LEAD + 1):
                fetch(m, m)
            clear().then_inc(S("summed"), CLEARED)
            with pe.Fori(0, q) as i:
                for u in range(RING):
                    step = i * RING + u
                    ends = load(pe, mybir.EngineType.PE, sched[0:1, 1, groups(step)], 1)
                    for g in range(GS):
                        if g == 0:
                            own_wait(pe, "z_ready", step + 1)
                            fetch(step + (LEAD + 1), (u + LEAD + 1) % RING)
                        own_wait(pe, "y_ready", step * GS + (g + 1))
                        add(sel[:, u, g, :], G[:, u, g, :]).then_inc(S("summed"), 1)
                        with pe.If(ends[g] > 0):
                            take(pe, "flushed")
                            clear()

            pe.wait_ge(S("flags_ready"), 1)
            some = pe.value_load(missi[0:1, NT:NT + 1], min_val=0, max_val=1)
            with pe.If(some > 0):
                with pe.Fori(0, NT) as t:
                    flagged = pe.value_load(missi[0:1, bass.ds(t, 1)], min_val=0, max_val=1)
                    with pe.If(flagged > 0):
                        take(pe, "t4_sign")
                        pack(sign4, psW)
                        clear().then_inc(S("t4_packed"), 1)
                        with pe.Fori(0, NCH):
                            take(pe, "t4_steps_pe")
                            steps = pe.value_load(steps4[0:1, 0:1], min_val=1, max_val=BITS * CW // 8)
                            with pe.Fori(0, steps):
                                take(pe, "t4_y")
                                for g in range(8):
                                    last = add(eye[:], G4[:, g, :])
                                last.then_inc(S("t4_summed"), 1)

        @block.vector
        def _(dve):
            ch = Chain(dve, "dve")
            cj = [Chain(dve, f"dve_job{j}") for j in range(3)]
            v_ = nc.vector
            v_.memset(epsc[:], 1e-5)
            v_.memset(halfc[:], -0.5)
            v_.memset(onec[:], 1.0)
            v_.memset(V[:], 0.0)
            v_.memset(cntstep[:], 0.0)
            v_.memset(nobody[:, 0:TR], 0.0)
            v_.memset(sched[:, :, 0:2 * GS], 0)
            v_.memset(zero[:], 0.0)
            v_.memset(zrow[:], 0.0)
            ch.step(v_.memset(awd[:], 0.0))
            v_.memset(halves(nobody[:], "scores"), FAR)
            dve.wait_ge(S("const_in"), 16 * len(const))
            dve.wait_ge(S("weights_in"), 64)
            for k in range(BITS):
                v_.tensor_scalar(packs[:, k, :], eye[:], float(WSC * 2 ** k), None, ALU.mult)
            v_.memset(ones2[:], 1.0)
            v_.tensor_copy(wordrow[:], C["wordrow"][:])
            v_.memset(cnt0[:], 0.0).then_inc(S("init"), 1)
            for o in range(KC):
                for half in range(2):
                    h = 2 * o + half
                    rows = slice(half * DH, (half + 1) * DH)
                    v_.tensor_copy(awd[rows, o, h:h + 1], aw2[rows, o, 0:1])
                    v_.tensor_copy(awd[rows, o, H + h:H + h + 1], aw2[rows, o, 1:2])
            v_.tensor_copy(biasrep[:], bcol[:].unsqueeze(2).to_broadcast([P, KC, P])).then_inc(S("awd_done"), 1)
            dve.wait_ge(S("wa_done"), 1)
            v_.tensor_copy(wa[:].rearrange("p c k -> p (c k)"), psA[:, 0:64])
            v_.tensor_copy(abias[:], psA[:, 64:80]).then_inc(S("bias_done"), 1)
            dve.wait_ge(S("bias_done"), 1)

            def means(t, k):
                for par in range(2):
                    dve.wait_ge(S(f"x_in{par}"), k)
                    cj[par].go(v_.bn_stats(stats[:, par, :], xt[:, par, :]))
                if not isinstance(t, int):
                    own_wait(dve, "sd_ready", t)
                for par in range(2):
                    cj[par].wait()
                    cj[par].go(v_.bn_aggr(mv[:, par, :], stats[:, par, :]))
                for par in range(2):
                    cj[par].wait()
                    v_.tensor_scalar(negm[:, par:par + 1], mv[:, par, 0:1], -1.0, None, ALU.mult).then_inc(S("mean_ready"), 1)

            def rows(t, k):
                own_wait(dve, "sd_ready", t + 2)
                ch.step(v_.reciprocal(rs[:], sd[:]))
                dve.wait_ge(S("hm_done"), t + 2)
                for par in range(2):
                    r1 = rs[:, par:par + 1]
                    if k is not None:
                        dve.wait_ge(S(f"row_out{par}"), k)
                    v_.scalar_tensor_tensor(ab[:, bass.ds(t + par, 1), :].rearrange("p a c -> p (a c)"),
                                            psS[:, 16 * par:16 * par + 16], r1, abias[:], ALU.mult, ALU.add)
                    v_.scalar_tensor_tensor(halves(trow[:, par, :], "scores"),
                                            psS[:, 16 * par + H:16 * par + 16].rearrange("p (a c) -> p a c", a=2), r1,
                                            abias[:, H:2 * H].rearrange("p (a c) -> p a c", a=2), ALU.mult, ALU.add)
                    v_.scalar_tensor_tensor(halves(trow[:, par, :], "values"),
                                            [psH[:], psA][par].rearrange("p (a c) -> p a c", a=2), r1,
                                            bias[:].rearrange("p (a c) -> p a c", a=2),
                                            ALU.mult, ALU.add).then_inc(S("row_ready"), 1)

            def chunked(words):
                return words.rearrange("p (w c) -> p c w", c=NCH)

            def candidates(jobs):
                for j, (src, nw) in jobs.items():
                    cj[j].go(v_.tensor_scalar(wint[:, j, 0:nw].unsqueeze(1) if len(src.shape) == 3 else wint[:, j, 0:nw],
                                              src, float(WSC * 255), None, ALU.add))
                for j, (src, nw) in jobs.items():
                    cj[j].wait()
                    v_.tensor_tensor(bits[:, j, :, 0:nw], wint[:, j, 0:nw].unsqueeze(1).to_broadcast([P, BITS, nw]),
                                     C["bitmask"][:].unsqueeze(2).to_broadcast([P, BITS, nw]), ALU.bitwise_and)
                    cj[j].go(v_.tensor_scalar(widx[:, j, 0:nw], wint[:, j, 0:nw], 2 * WSC - 1, None, ALU.bitwise_and))
                for j, (src, nw) in jobs.items():
                    cj[j].wait()
                    cj[j].go(v_.tensor_scalar(wneg[:, j, 0:nw], widx[:, j, 0:nw], -1.0, float(TOP), ALU.mult, ALU.add))
                for j, (src, nw) in jobs.items():
                    cj[j].wait()
                    cj[j].go(v_.tensor_tensor(cand[:, j, :, 0:nw], wneg[:, j, 0:nw].unsqueeze(1).to_broadcast([P, BITS, nw]),
                                              C["bitcol"][:].unsqueeze(2).to_broadcast([P, BITS, nw]), ALU.subtract))
                for j, (src, nw) in jobs.items():
                    cj[j].wait()
                    cj[j].go(v_.scalar_tensor_tensor(cand[:, j, :, 0:nw], bits[:, j, :, 0:nw], 0.0, cand[:, j, :, 0:nw],
                                                     ALU.is_gt, ALU.mult))

            def lists(tiles, rounds, chunk=None):
                for j, t in tiles.items():
                    own_wait(dve, "packed", t + 1)
                    words = chunked([psW, psV][j][:, 0:NW])
                    for c in range(NCH):
                        last = v_.max(tops[:, j, 8 * c:8 * c + 8], words[:, c, :])
                    last.then_inc(S("words_used"), 1)
                for r in range(rounds):
                    for j, t in tiles.items():
                        if r == 0:
                            own_wait(dve, "words_used", t + 1)
                        else:
                            cj[j].wait()
                        cj[j].go(v_.max(wl[:, j, 8 * r:8 * r + 8], tops[:, j, :]))
                    if r < rounds - 1:
                        for j in tiles:
                            cj[j].wait()
                            cj[j].go(v_.match_replace(tops[:, j, :], wl[:, j, 8 * r:8 * r + 8], tops[:, j, :], GONE))
                for j in tiles:
                    cj[j].wait()
                jobs = {j: (wl[:, j, 0:8 * rounds], 8 * rounds) for j in tiles}
                depth = {j: rounds for j in tiles}
                slot = {j: t + (NCH - 1) for j, t in tiles.items()}
                if chunk is not None:
                    jobs[2] = (chunked(words0[:])[:, bass.ds(chunk, 1), :], CW)
                    depth[2], slot[2] = FIRST, chunk
                candidates(jobs)
                for r in range(max(depth.values())):
                    for j, (src, nw) in jobs.items():
                        if r < depth[j]:
                            cj[j].wait()
                            cj[j].go(v_.max(lst[:, j, 8 * r:8 * r + 8], cand[:, j, :, 0:nw]))
                    for j, (src, nw) in jobs.items():
                        if r < depth[j] - 1:
                            cj[j].wait()
                            cj[j].go(v_.match_replace(cand[:, j, :, 0:nw], lst[:, j, 8 * r:8 * r + 8], cand[:, j, :, 0:nw], 0.0))
                for j in jobs:
                    cj[j].wait()
                    v_.tensor_copy(V[:, bass.ds(slot[j], 1), 18:18 + 8 * depth[j]].rearrange("p a c -> p (a c)"),
                                   lst[:, j, 0:8 * depth[j]])

            means(0, 16)
            rows(0, None)
            dve.wait_ge(S("packed"), 1)
            v_.tensor_copy(words0[:], psW[:, 0:NW]).then_inc(S("words_used"), 1)
            dve.wait_ge(S("words_used"), 1)
            means(2, 32)
            lists({1: 1}, SECOND)

            def pair(t, k, rounds, chunk=None, more=True):
                rows(t, k - 16)
                if more:
                    means(t + 2, k + 16)
                lists({0: t, 1: t + 1}, rounds, chunk)

            pair(2, 32, SECOND)
            with dve.Fori(0, (LATE_FROM - MIDDLE_FROM) // 2) as i:
                pair(i * 2 + MIDDLE_FROM, i * 16 + 8 * (MIDDLE_FROM + 2), MIDDLE)
            with dve.Fori(0, NCH) as i:
                pair(i * 2 + LATE_FROM, i * 16 + 8 * (LATE_FROM + 2), LATE, i)
            for t in range(LATE_FROM + 2 * NCH, NT, 2):
                pair(t, 8 * (t + 2), LATE, None, t + 2 < NT)

            ch.step(v_.tensor_reduce(bmax1[:], ab[:, :, H:2 * H].rearrange("p t h -> p h t"), AX.X, ALU.max))
            dve.wait_ge(S("sign_done"), NT)
            dve.wait_ge(S("packed"), NT)
            for a in acc:
                v_.memset(halves(a, "scores"), 1.0)
            ones4 = aj[:, 0, 0:NV * K].bitcast(f32).rearrange("p (v k) -> p v k", k=K)
            ch.step(v_.tensor_scalar(ones4, V[:, 0:NV, 18:VC], 0.0, None, ALU.is_gt))
            ch.step(v_.tensor_reduce(cnt[:], ones4, AX.X, ALU.add))
            v_.tensor_tensor(cntstep[:, 0:NV - 1], cnt[:, 1:NV], cnt[:, 0:NV - 1], ALU.subtract).then_inc(S("s2"), 1)
            ch.step(v_.tensor_reduce(cnt0[:], cnt[:, 0:NCH], AX.X, ALU.add))
            ch.step(v_.tensor_scalar(miss[:, 0:NT], signsum[:], 0.5, float(N // 2), ALU.mult, ALU.add))
            v_.tensor_tensor(miss[:, 0:1], miss[:, 0:1], cnt0[:], ALU.subtract)
            ch.step(v_.tensor_tensor(miss[:, 1:NT], miss[:, 1:NT], cnt[:, NCH:NV], ALU.subtract))
            v_.tensor_reduce(miss[:, NT:NT + 1], miss[:, 0:NT], AX.X, ALU.max).then_inc(S("lists_done"), 1)
            dve.wait_ge(S("s2pe"), 1)
            ch.step(v_.tensor_scalar(nbi[:], psH[0:NV, 0:1], float(P - 1), None, ALU.add))
            ch.step(v_.tensor_scalar(nbi[:], nbi[:], P.bit_length() - 1, None, ALU.arith_shift_right))
            ch.step(v_.tensor_copy(nb[:], nbi[:]))
            ch.step(v_.tensor_tensor(nb[:], nb[:], C["newrow"][:], ALU.max))
            v_.tensor_copy(nbrep[:], nb[:].to_broadcast([NV, P]))
            ch.step(v_.scalar_tensor_tensor(steplhs[:], nb[:].to_broadcast([NV, P]), float(P), psY[0:NV, 0:P],
                                            ALU.mult, ALU.add))
            ch.step(v_.tensor_copy(stephigh[:], steplhs[:]))
            v_.tensor_copy(newrow16[:], C["newrow"][:])
            v_.memset(ones16[:], 1.0)
            v_.tensor_tensor(steplow[:], steplhs[:], stephigh[:], ALU.subtract).then_inc(S("s2"), 1)
            ch.step(v_.tensor_copy(starts[:, 0:NV], psT[:, 0:NV]))
            v_.tensor_scalar(groupbase[:], C["count"][:, 0:SW], float(-P), starts[:, 0:1], ALU.mult, ALU.add)
            v_.tensor_copy(V[:, 0:NV, 0:1].rearrange("p v c -> p (v c)"), starts[:, 0:NV])
            v_.tensor_copy(V[:, 0:NV, 1:2].rearrange("p v c -> p (v c)"), C["row1"][:].to_broadcast([P, NV]))
            v_.tensor_copy(V[:, 0:NCH, 2:2 + H], ab[:, 0:1, 0:H].to_broadcast([P, NCH, H]))
            v_.tensor_copy(V[:, NCH:NV, 2:2 + H], ab[:, 1:NT, 0:H])
            dve.wait_ge(S("bmax_done"), 1)
            ch.step(v_.tensor_tensor(bound[:], ab[:, :, 0:H], bmax[:].unsqueeze(1).to_broadcast([P, NT, H]), ALU.add))
            ch.step(v_.scalar_tensor_tensor(bound[:], bound[:], ALPHA, bound[:], ALU.mult, ALU.max))
            ch.step(v_.tensor_scalar(bound[:], bound[:], -HEADROOM, None, ALU.add))
            v_.tensor_copy(V[:, 0:NCH, 2 + H:2 + 2 * H], bound[:, 0:1, :].to_broadcast([P, NCH, H]))
            v_.tensor_copy(V[:, NCH:NV, 2 + H:2 + 2 * H], bound[:, 1:NT, :]).then_inc(S("s2"), 1)
            dve.wait_ge(S("s2pe"), 2)
            ch.step(v_.tensor_copy(cum[:], psX[0:NV, 0:1]))
            ch.step(v_.tensor_scalar(iters[:], psX[0:1, 1:2], float(RING * GS - 1), None, ALU.add))
            ch.step(v_.tensor_scalar(iters[:], iters[:], (RING * GS).bit_length() - 1, None, ALU.arith_shift_right))
            for g in range(8):
                dve.wait_ge(S("diffs"), g + 1)
                v_.tensor_copy(Dv[:, 8 * g:8 * g + 8, :].rearrange("p v c -> p (v c)"),
                               [psA, psS][g % 2][:, 0:8 * VC]).then_inc(S("diffs_used"), 1)
            for j in range(NMAX // SW):
                v_.tensor_scalar(reachn, C["count"][0:NV, 0:SW], float(j * SW), cum[:], ALU.add, ALU.is_ge)
                v_.tensor_scalar(endsn, C["count"][0:NV, 1:SW + 1], float(j * SW), cum[:], ALU.add,
                                 ALU.is_equal).then_inc(S("s2"), 1)
                dve.wait_ge(S("s2pe"), 3 + j)
                v_.tensor_copy(sched[0:1, 0, 2 * GS + j * SW:2 * GS + (j + 1) * SW], psT[0:1, 0:SW])
                v_.tensor_copy(sched[0:1, 1, 2 * GS + j * SW:2 * GS + (j + 1) * SW], psH[0:1, 0:SW])
                v_.scalar_tensor_tensor(startof[:, j * SW:(j + 1) * SW], psX[:, 0:SW], float(-P * SW * j),
                                        groupbase[:], ALU.add, ALU.add)
                last = v_.scalar_tensor_tensor(batchof[:, j * SW:(j + 1) * SW], C["count"][:, 0:SW], float(SW * j),
                                               psY[:, 0:SW], ALU.add, ALU.subtract)
            last.then_inc(S("sched_done"), 1)
            dve.wait_ge(S("sched_done"), 1)

            q = dve.value_load(iters[0:1, 0:1], min_val=1, max_val=QMAX)

            def fetched(u):
                return fetchd[u][:, 0:GS * VC].rearrange("p (g c) -> p g c", g=GS)

            def rank_of(step, u):
                own_wait(dve, "fetched", step + 1)
                cj[0].go(v_.scalar_tensor_tensor(rank[:], batchof[:, bass.ds(step * GS, GS)], float(P), fetched(u)[:, :, 0],
                                                 ALU.mult, ALU.subtract))

            def hit_of():
                cj[0].wait()
                cj[0].go(v_.tensor_tensor(hit[:], C["rankoff"][:].unsqueeze(1).to_broadcast([P, GS, K]),
                                          rank[:].unsqueeze(2).to_broadcast([P, GS, K]), ALU.is_equal))

            def pick_of(u):
                cj[0].wait()
                cj[0].go(v_.tensor_tensor(hit[:], hit[:], fetched(u)[:, :, 18:VC], ALU.mult))

            def value_of():
                cj[0].wait()
                cj[0].go(v_.tensor_reduce(val[:], hit[:], AX.X, ALU.add))

            def index(u):
                cj[0].wait()
                v_.tensor_scalar(idx[:, u, :], val[:], -1.0, float(TOP), ALU.mult, ALU.add).then_inc(S("idx_ready"), 1)
                cj[0].go(v_.scalar_tensor_tensor(node1[:], val[:], 0.0, fetched(u)[:, :, 1], ALU.is_gt, ALU.mult))

            def select(u):
                cj[0].wait()
                v_.tensor_tensor(sel[:, u, :, :], C["count"][:, 1:P + 1].unsqueeze(1).to_broadcast([P, GS, P]),
                                 node1[:].unsqueeze(2).to_broadcast([P, GS, P]), ALU.is_equal)

            def score_sum(u, gathers):
                dve.wait_ge(S(f"g_in{u}"), gathers)
                cj[1].go(v_.tensor_tensor(z2[:].rearrange("p g (a c) -> p g a c", a=2), halves(G[:, u], "scores"),
                                          fetched(u)[:, :, 2:2 + H].rearrange("p g (a c) -> p g a c", a=2), ALU.add))

            def score_relu():
                cj[1].wait()
                cj[1].go(v_.scalar_tensor_tensor(z2[:], z2[:], ALPHA, z2[:], ALU.mult, ALU.max))

            def score_below(u):
                cj[1].wait()
                v_.tensor_tensor(z[:], z2[:], fetched(u)[:, :, 2 + H:2 + 2 * H], ALU.subtract).then_inc(S("z_ready"), 1)

            def den_floor(step, par):
                own_wait(dve, "saved", step + 1)
                cj[2].go(v_.tensor_scalar(denmax[:].rearrange("p g (a c) -> p g a c", a=2), halves(acc[par], "scores"),
                                          1e-37, None, ALU.max))

            def den_inverse(step, u):
                own_wait(dve, "finished", step + 1)
                cj[2].wait()
                v_.reciprocal(rdens[:, u % 2, :, :], denmax[:]).then_inc(S("rden_ready"), 1)

            def weigh(row):
                y = halves(row, "values").rearrange("p a (h d) -> p a h d", d=DH)
                return v_.tensor_tensor(y, y, halves(row, "scores").unsqueeze(3).to_broadcast([P, 2, H // 2, DH]), ALU.mult)

            dve.sem_inc(S("rden_ready"), 2)
            for m in range(LEAD):
                rank_of(m, m)
                hit_of()
                pick_of(m)
                value_of()
                index(m)
                select(m)
            score_sum(0, 16 * GS)
            score_relu()
            score_below(0)
            with dve.Fori(0, q) as i:
                for u in range(RING):
                    step = i * RING + u
                    new, soon = (u + LEAD) % RING, (u + 1) % RING
                    rank_of(step + LEAD, new)
                    dve.wait_ge(S("prob_ready"), step + 1)
                    weigh(G[:, u, 0, :]).then_inc(S("y_ready"), 1)
                    hit_of()
                    weigh(G[:, u, 1, :]).then_inc(S("y_ready"), 1)
                    pick_of(new)
                    score_sum(soon, i * (16 * GS) + (16 * GS if u < RING - 1 else 32 * GS))
                    weigh(G[:, u, 2, :]).then_inc(S("y_ready"), 1)
                    value_of()
                    score_relu()
                    weigh(G[:, u, 3, :]).then_inc(S("y_ready"), 1)
                    score_below(soon)
                    own_wait(dve, "summed", step * GS + CLEARED)
                    index(new)
                    den_floor(step, u % 2)
                    select(new)
                    den_inverse(step, u)
            own_wait(dve, "rden_ready", q * RING + 2)
            den_floor(q * RING, 0)
            den_inverse(q * RING, 0)

            dve.wait_ge(S("flags_ready"), 1)
            dve.wait_ge(S("drained"), 1)
            rows_in = Landed(dve, "t4_rows", 8 * 16)
            x_in = Landed(dve, "t4_x", 16)
            some = dve.value_load(missi[0:1, NT:NT + 1], min_val=0, max_val=1)
            with dve.If(some > 0):
                with dve.Fori(0, NT) as t:
                    flagged = dve.value_load(missi[0:1, bass.ds(t, 1)], min_val=0, max_val=1)
                    with dve.If(flagged > 0):
                        take(dve, "t4_packed")
                        with dve.Fori(0, NCH) as c:
                            candidates({0: (chunked(psW[:, 0:NW])[:, bass.ds(c, 1), :], CW)})
                            cj[0].wait()
                            ch.step(v_.tensor_scalar(bits[:, 0], cand[:, 0], 0.0, None, ALU.is_gt))
                            v_.tensor_reduce(count4[:], bits[:, 0].rearrange("p k w -> p (k w)"), AX.X,
                                             ALU.add).then_inc(S("t4_count"), 1)
                            take(dve, "t4_most")
                            ch.step(v_.tensor_scalar(steps4[:], most[0:1, :], 1.0, 7.0, ALU.max, ALU.add))
                            ch.step(v_.tensor_scalar(steps4[:], steps4[:], 3, None, ALU.arith_shift_right))
                            for name in ("t4_steps_pe", "t4_steps_act", "t4_steps_pool"):
                                dve.sem_inc(S(name), 1)
                            steps = dve.value_load(steps4[0:1, 0:1], min_val=1, max_val=BITS * CW // 8)
                            with dve.Fori(0, steps):
                                ch.step(v_.max(l8[:], cand[:, 0]))
                                v_.tensor_scalar(idx8[:], l8[:], -1.0, float(TOP), ALU.mult, ALU.add).then_inc(S("t4_idx"), 1)
                                ch.step(v_.match_replace(cand[:, 0], l8[:], cand[:, 0], 0.0))
                                rows_in.wait()
                                ch.step(v_.tensor_tensor(z8[:].rearrange("p g (a c) -> p g a c", a=2), halves(G4, "scores"),
                                                         ab[:, bass.ds(t, 1), 0:H].rearrange("p g (a c) -> p g a c", a=2).to_broadcast([P, 8, 2, H // 2]), ALU.add))
                                ch.step(v_.scalar_tensor_tensor(z8[:], z8[:], ALPHA, z8[:], ALU.mult, ALU.max))
                                v_.tensor_tensor(z8[:], z8[:], bound[:, bass.ds(t, 1), :].to_broadcast([P, 8, H]),
                                                 ALU.subtract).then_inc(S("t4_z"), 1)
                                take(dve, "t4_prob")
                                for g in range(8):
                                    last = weigh(G4[:, g, :])
                                last.then_inc(S("t4_y"), 1)
                                take(dve, "t4_summed")
                        ch.step(v_.tensor_scalar(den[:].rearrange("p (a c) -> p a c", a=2), psAD[:, :, D // 2:HALF], 1e-37, None, ALU.max))
                        ch.step(v_.reciprocal(rden[:], den[:]))
                        x_in.wait()
                        ch.step(v_.tensor_tensor(ob[:].rearrange("p (a h d) -> p a h d", a=2, d=DH),
                                                 psAD[:, :, 0:D // 2].rearrange("p a (h d) -> p a h d", d=DH),
                                                 rden[:].rearrange("p (a h) -> p a h", a=2).unsqueeze(3).to_broadcast([P, 2, H // 2, DH]), ALU.mult))
                        v_.tensor_tensor(ob[:], ob[:], xo[:], ALU.add).then_inc(S("t4_out"), 1)

        @block.gpsimd
        def _(pool):
            with pool.Fori(0, NT // 2) as i:
                for par in range(2):
                    own_wait(pool, "row_ready", i * 2 + (par + 1))
                    nc.gpsimd.dma_start(table[bass.ds(i * (2 * P) + par * P, P), :], trow[:, par, :]).then_inc(S(f"row_out{par}"), 16)
            pool.wait_ge(S("lists_done"), 1)
            nc.gpsimd.partition_all_reduce(bmax[:], bmax1[:], P, bass.bass_isa.ReduceOp.max).then_inc(S("bmax_done"), 1)
            nc.gpsimd.partition_all_reduce(missmax[:], miss[:], P, bass.bass_isa.ReduceOp.max).then_inc(S("pool"), 1)
            pool.wait_ge(S("pool"), 1)
            nc.gpsimd.tensor_scalar(missi[:], missmax[:], 0.0, None, ALU.is_gt).then_inc(S("flags_ready"), 1)
            pool.wait_ge(S("flags_ready"), 1)
            for par in range(2):
                pool.wait_ge(S(f"row_out{par}"), 16 * NT // 2)
            pool.wait_ge(S("sched_done"), 1)
            q = pool.value_load(iters[0:1, 0:1], min_val=1, max_val=QMAX)

            def gather(step, u):
                own_wait(pool, "idx_ready", step + 1)
                for g in range(GS):
                    nc.gpsimd.indirect_dma_start(
                        out=G[:, u, g, :], out_offset=None, in_=table,
                        in_offset=bass.IndirectOffsetOnAxis(ap=idx[:, u, g:g + 1], axis=0),
                        bounds_check=TOP, oob_is_err=False).then_inc(S(f"g_in{u}"), 16)

            link = Chain(pool, "final").step

            def finish(step, u):
                ends = load(pool, mybir.EngineType.Pool, sched[0:1, 1, groups(step, 2)], 1)
                for g in range(GS):
                    with pool.If(ends[g] > 0):
                        own_wait(pool, "rden_ready", step + 2)
                        take(pool, "x_there")
                        link(nc.gpsimd.tensor_tensor(ob[:].rearrange("p (a h d) -> p a h d", a=2, d=DH),
                                                     halves(acc[(u + 1) % 2][:, g, :], "values").rearrange("p a (h d) -> p a h d", d=DH),
                                                     rdens[:, (u + 1) % 2, g, :].rearrange("p (a h) -> p a h", a=2).unsqueeze(3).to_broadcast([P, 2, H // 2, DH]),
                                                     ALU.mult))
                        nc.gpsimd.tensor_tensor(ob[:], ob[:], xo[:], ALU.add).then_inc(S("out_ready"), 1)
                pool.sem_inc(S("finished"), 1)

            pool.wait_ge(S("nobody_out"), 16)
            pool.sem_inc(S("finished"), 1)
            for m in range(LEAD):
                gather(m, m)
            with pool.Fori(0, q) as i:
                for u in range(RING):
                    finish(i * RING + u, u)
                    gather(i * RING + (u + LEAD), (u + LEAD) % RING)
            finish(q * RING, 0)
            finish(q * RING + 1, 1)
            for m in range(LEAD):
                own_wait(pool, f"g_in{m}", q * (16 * GS) + 16 * GS)
            own_wait(pool, "summed", q * (RING * GS) + CLEARED)
            own_wait(pool, "rden_ready", q * RING + 3)
            pool.sem_inc(S("drained"), 1)

            some = pool.value_load(missi[0:1, NT:NT + 1], min_val=0, max_val=1)
            with pool.If(some > 0):
                with pool.Fori(0, NT) as t:
                    flagged = pool.value_load(missi[0:1, bass.ds(t, 1)], min_val=0, max_val=1)
                    with pool.If(flagged > 0):
                        with pool.Fori(0, NCH):
                            take(pool, "t4_count")
                            nc.gpsimd.partition_all_reduce(most[:], count4[:], P, bass.bass_isa.ReduceOp.max).then_inc(S("t4_most"), 1)
                            take(pool, "t4_steps_pool")
                            steps = pool.value_load(steps4[0:1, 0:1], min_val=1, max_val=BITS * CW // 8)
                            with pool.Fori(0, steps):
                                take(pool, "t4_idx")
                                for g in range(8):
                                    nc.gpsimd.indirect_dma_start(
                                        out=G4[:, g, :], out_offset=None, in_=table,
                                        in_offset=bass.IndirectOffsetOnAxis(ap=idx8[:, g:g + 1], axis=0),
                                        bounds_check=TOP, oob_is_err=False).then_inc(S("t4_rows"), 16)


_INS = ["x", "adj", "L0_gnn_W", "L0_gnn_b", "L0_gnn_aw"]
_OUTS = [((N, D), "float32")]


def kernel(**inputs):
    import numpy as _np
    import concourse.bacc as _bacc
    from concourse import mybir as _mybir
    from concourse.bass_utils import run_bass_kernel_spmd as _run

    nc = _bacc.Bacc("TRN2", target_bir_lowering=False, num_devices=1)
    arrays, args, const = {}, [], {}
    for name in _INS:
        a = _np.ascontiguousarray(inputs[name])
        arrays[f"in_{name}_dram"] = a
        args.append(nc.dram_tensor(f"in_{name}_dram", a.shape, _mybir.dt.from_np(a.dtype), kind="ExternalInput").ap())
    for name, a in constants().items():
        arrays[f"const_{name}_dram"] = a
        const[name] = nc.dram_tensor(f"const_{name}_dram", a.shape, _mybir.dt.from_np(a.dtype), kind="ExternalInput").ap()
    outs = []
    for i, (shape, dtype) in enumerate(_OUTS):
        dt = _mybir.dt.from_np(_np.dtype(dtype))
        outs.append(nc.dram_tensor(f"out_{i}_dram", shape, dt, kind="ExternalOutput").ap())
    build(nc, *args, const, *outs)
    r = _run(nc, [arrays], core_ids=[0])
    got = tuple(r.results[0][f"out_{i}_dram"] for i in range(len(_OUTS)))
    return got[0]
```
